# Optimizing a Trainium2 kernel written in Bass

```python
import numpy as np
import jax
import jax.numpy as jnp

def _softmax(x, axis=-1):
    return jax.nn.softmax(x, axis=axis)

def _gelu(x):
    return jax.nn.gelu(x, approximate=True)

def _silu(x):
    return jax.nn.silu(x)

def _sigmoid(x):
    return jax.nn.sigmoid(x)

def _layernorm(x, axis=-1, eps=1e-05):
    m = jnp.mean(x, axis=axis, keepdims=True)
    v = jnp.var(x, axis=axis, keepdims=True)
    return (x - m) / jnp.sqrt(v + eps)

def _scatter_add(tgt, idx, src, axis=0):
    return tgt.at[idx].add(src)

def _segment_sum(src, seg, n):
    return jax.ops.segment_sum(src, seg, n)
kernel_name = 'mk_xattn_seq_d4_seqx_r8_e08bea'

def setup_inputs(seed: int=0):
    np.random.seed(seed)
    _w = jnp.asarray

    def _rec_inputs():
        import jax
        import jax.numpy as jnp
        _rk = jax.random.key(seed)
        x = -0.000125 + 0.9999 * jax.random.normal(jax.random.fold_in(_rk, 1), (8, 128, 256), jnp.float32)
        _lenS = 128 - jax.random.randint(jax.random.fold_in(_rk, 7), (8,), 0, max(1, 128 // 4) + 1, jnp.int32)
        _lenS2 = 128 - jax.random.randint(jax.random.fold_in(_rk, 8), (8,), 0, max(1, 128 // 4) + 1, jnp.int32)
        _ctx_1024P = jax.random.normal(jax.random.fold_in(_rk, 11), (8, 16, 128), jnp.float32)
        _ctx_1024c = jax.random.dirichlet(jax.random.fold_in(_rk, 511), 0.3 * jnp.ones((16,), jnp.float32), (8, 128))
        _ctx_1024t = jnp.einsum('bsk,bkd->bsd', _ctx_1024c, _ctx_1024P)
        _ctx_1024t = _ctx_1024t * jax.lax.rsqrt(jnp.mean(jnp.square(_ctx_1024t)) + 1e-12) * 0.953939
        ctx_1024 = 4.13588e-05 + 0.999923 * (_ctx_1024t + 0.3 * jax.random.normal(jax.random.fold_in(_rk, 611), (8, 128, 128), jnp.float32))
        pos_1xS = jnp.broadcast_to(jnp.arange(128, dtype=jnp.int32), (1, 128))
        _validS = jnp.arange(128)[None, :] < _lenS[:, None]
        _validS2 = jnp.arange(128)[None, :] < _lenS2[:, None]
        _causal = jnp.tril(jnp.ones((128, 128), dtype=bool))
        mask_BxS2_bk0 = jnp.logical_not(jnp.broadcast_to(_validS2[:, :], (8, 128)))
        mask_BxS_ik0 = jnp.where(jnp.broadcast_to(_validS[:, :], (8, 128)), 0, 1).astype(jnp.int32)
        return (x, ctx_1024, pos_1xS, mask_BxS2_bk0, mask_BxS_ik0)
    x, ctx_1024, pos_1xS, mask_BxS2_bk0, mask_BxS_ik0 = _rec_inputs()

    def _L0_xattn_setup():
        import jax, jax.numpy as jnp
        import numpy as np
        EPS = 1e-06

        def _rmsnorm(x, w):
            var = jnp.mean(jnp.square(x), axis=-1, keepdims=True)
            return x * jax.lax.rsqrt(var + EPS) * w
        key = jax.random.key(seed)
        ks = jax.random.split(key, 6)
        B, N, M = (4, 512, 256)
        d_model, memory_dim = (256, 128)
        hidden_states = jax.random.normal(ks[0], (B, N, d_model), dtype=jnp.float32)
        memory = jax.random.normal(ks[1], (B, M, memory_dim), dtype=jnp.float32)
        W_mem = jax.random.normal(ks[2], (d_model, memory_dim), dtype=jnp.float32) / np.sqrt(memory_dim)
        W_gate = jax.random.normal(ks[3], (d_model, 2 * d_model), dtype=jnp.float32) / np.sqrt(2 * d_model)
        b_gate = jax.random.normal(ks[4], (d_model,), dtype=jnp.float32) * 0.01
        norm_w = jnp.ones((d_model,), dtype=jnp.float32)
        return {'hidden_states': hidden_states, 'memory': memory, 'W_mem': W_mem, 'W_gate': W_gate, 'b_gate': b_gate, 'norm_w': norm_w}
    _L0_xattn_all = _L0_xattn_setup()
    _L0_xattn_in = {k: v for k, v in _L0_xattn_all.items() if k in ('W_mem', 'W_gate', 'b_gate', 'norm_w')}
    del _L0_xattn_all

    def _L1_xattn_setup():
        import jax, jax.numpy as jnp
        import numpy as np
        DIM = 256
        DIM_MEDIA = 128
        HEADS = 16
        DIM_HEAD = 64
        INNER = HEADS * DIM_HEAD
        FF_INNER = 4 * DIM
        B, N_TOK, N_LAT = (4, 256, 64)
        EPS = 1e-05

        def layernorm(x, g, b):
            mu = jnp.mean(x, axis=-1, keepdims=True)
            var = jnp.var(x, axis=-1, keepdims=True)
            return (x - mu) * jax.lax.rsqrt(var + EPS) * g + b
        key = jax.random.key(seed)
        ks = jax.random.split(key, 12)
        x = jax.random.normal(ks[0], (B, N_TOK, DIM), dtype=jnp.float32)
        media = jax.random.normal(ks[1], (B, N_LAT, DIM_MEDIA), dtype=jnp.float32)
        media_mask = jax.random.randint(ks[2], (B, N_LAT), 0, 2).astype(bool)
        media_mask = media_mask.at[:, 0].set(True)
        s = lambda d: 1.0 / np.sqrt(d)
        Wq = jax.random.normal(ks[3], (DIM, INNER), dtype=jnp.float32) * s(DIM)
        Wkv = jax.random.normal(ks[4], (DIM_MEDIA, 2 * INNER), dtype=jnp.float32) * s(DIM_MEDIA)
        Wo = jax.random.normal(ks[5], (INNER, DIM), dtype=jnp.float32) * s(INNER)
        W1 = jax.random.normal(ks[6], (DIM, FF_INNER), dtype=jnp.float32) * s(DIM)
        W2 = jax.random.normal(ks[7], (FF_INNER, DIM), dtype=jnp.float32) * s(FF_INNER)
        return {'x': x, 'media': media, 'media_mask': media_mask, 'ln_q_g': jnp.ones((DIM,), jnp.float32), 'ln_q_b': jnp.zeros((DIM,), jnp.float32), 'Wq': Wq, 'Wkv': Wkv, 'Wo': Wo, 'attn_gate': jax.random.normal(ks[8], (1,), jnp.float32) * 0.5, 'ln_ff_g': jnp.ones((DIM,), jnp.float32), 'ln_ff_b': jnp.zeros((DIM,), jnp.float32), 'W1': W1, 'W2': W2, 'ff_gate': jax.random.normal(ks[9], (1,), jnp.float32) * 0.5}
    _L1_xattn_all = _L1_xattn_setup()
    _L1_xattn_in = {k: v for k, v in _L1_xattn_all.items() if k in ('ln_q_g', 'ln_q_b', 'Wq', 'Wkv', 'Wo', 'attn_gate', 'ln_ff_g', 'ln_ff_b', 'W1', 'W2', 'ff_gate')}
    del _L1_xattn_all

    def _L2_xattn_setup():
        import jax, jax.numpy as jnp
        import numpy as np
        H = 256
        NH = 16
        HD = H // NH
        CH = 128
        CC = 128
        CHD = CC // NH
        I = 688
        B = 2
        L = 256
        LE = 128
        EPS = 1e-06

        def rms_norm(x, w):
            xf = x.astype(jnp.float32)
            var = jnp.mean(xf * xf, axis=-1, keepdims=True)
            return (w * (xf * jax.lax.rsqrt(var + EPS))).astype(x.dtype)

        def expert_mask(tt):
            vm = jnp.zeros(tt.shape, dtype=bool)
            vm = vm.at[:, :-1].set((tt[:, :-1] == 1) & (tt[:, 1:] == 1))
            return vm

        def rotate_half(x):
            d = x.shape[-1] // 2
            return jnp.concatenate([-x[..., d:], x[..., :d]], axis=-1)

        def apply_rotary(q, k, position_ids, seq_len):
            inv = 1.0 / 10000.0 ** (jnp.arange(0, HD, 2, dtype=jnp.float32) / HD)
            t = jnp.arange(seq_len, dtype=jnp.float32)
            freqs = jnp.outer(t, inv)
            emb = jnp.concatenate([freqs, freqs], axis=-1)
            cos = jnp.cos(emb)[position_ids][:, None].astype(q.dtype)
            sin = jnp.sin(emb)[position_ids][:, None].astype(q.dtype)
            return (q * cos + rotate_half(q) * sin, k * cos + rotate_half(k) * sin)

        def sdpa(q, k, v, causal):
            scale = 1.0 / np.sqrt(q.shape[-1])
            scores = jnp.einsum('bhqd,bhkd->bhqk', q * scale, k)
            if causal:
                mask = jnp.tril(jnp.ones((q.shape[-2], k.shape[-2]), dtype=bool))
                scores = jnp.where(mask, scores, jnp.finfo(jnp.float32).min)
            p = jax.nn.softmax(scores.astype(jnp.float32), axis=-1).astype(q.dtype)
            return jnp.einsum('bhqk,bhkd->bhqd', p, v)

        def heads(x, nh, hd):
            b, l, _ = x.shape
            return x.reshape(b, l, nh, hd).transpose(0, 2, 1, 3)
        key = jax.random.key(seed)
        ks = jax.random.split(key, 20)
        s = 0.02
        f32 = jnp.float32
        return {'hidden_states': jax.random.normal(ks[0], (B, L, H), f32), 'encoder_outputs': jax.random.normal(ks[1], (B, LE, CH), f32), 'token_type_ids': jax.random.randint(ks[2], (B, L), 0, 2, jnp.int32), 'position_ids': jnp.arange(L, dtype=jnp.int32)[None, :], 'ln_in_w': jnp.ones((H,), f32), 'ln_post_attn_w': jnp.ones((H,), f32), 'ln_post_cross_w': jnp.ones((H,), f32), 'v_qkv': jax.random.normal(ks[3], (H, 3 * H), f32) * s, 'l_qkv': jax.random.normal(ks[4], (H, 3 * H), f32) * s, 'v_dense': jax.random.normal(ks[5], (H, H), f32) * s, 'l_dense': jax.random.normal(ks[6], (H, H), f32) * s, 'cq_w': jax.random.normal(ks[7], (H, CC), f32) * s, 'ckv_w': jax.random.normal(ks[8], (CH, 2 * CC), f32) * s, 'cdense_w': jax.random.normal(ks[9], (CC, H), f32) * s, 'v_gate': jax.random.normal(ks[10], (H, I), f32) * s, 'v_up': jax.random.normal(ks[11], (H, I), f32) * s, 'v_down': jax.random.normal(ks[12], (I, H), f32) * s, 'l_gate': jax.random.normal(ks[13], (H, I), f32) * s, 'l_up': jax.random.normal(ks[14], (H, I), f32) * s, 'l_down': jax.random.normal(ks[15], (I, H), f32) * s}
    _L2_xattn_all = _L2_xattn_setup()
    _L2_xattn_in = {k: v for k, v in _L2_xattn_all.items() if k in ('ln_in_w', 'ln_post_attn_w', 'ln_post_cross_w', 'v_qkv', 'l_qkv', 'v_dense', 'l_dense', 'cq_w', 'ckv_w', 'cdense_w', 'v_gate', 'v_up', 'v_down', 'l_gate', 'l_up', 'l_down')}
    del _L2_xattn_all

    def _L3_xattn_setup():
        import jax, jax.numpy as jnp
        import numpy as np
        DIM = 256
        DIM_MEDIA = 128
        HEADS = 16
        DIM_HEAD = 64
        INNER = HEADS * DIM_HEAD
        FF_INNER = 4 * DIM
        B, N_TOK, N_LAT = (4, 256, 64)
        EPS = 1e-05

        def layernorm(x, g, b):
            mu = jnp.mean(x, axis=-1, keepdims=True)
            var = jnp.var(x, axis=-1, keepdims=True)
            return (x - mu) * jax.lax.rsqrt(var + EPS) * g + b
        key = jax.random.key(seed)
        ks = jax.random.split(key, 12)
        x = jax.random.normal(ks[0], (B, N_TOK, DIM), dtype=jnp.float32)
        media = jax.random.normal(ks[1], (B, N_LAT, DIM_MEDIA), dtype=jnp.float32)
        media_mask = jax.random.randint(ks[2], (B, N_LAT), 0, 2).astype(bool)
        media_mask = media_mask.at[:, 0].set(True)
        s = lambda d: 1.0 / np.sqrt(d)
        Wq = jax.random.normal(ks[3], (DIM, INNER), dtype=jnp.float32) * s(DIM)
        Wkv = jax.random.normal(ks[4], (DIM_MEDIA, 2 * INNER), dtype=jnp.float32) * s(DIM_MEDIA)
        Wo = jax.random.normal(ks[5], (INNER, DIM), dtype=jnp.float32) * s(INNER)
        W1 = jax.random.normal(ks[6], (DIM, FF_INNER), dtype=jnp.float32) * s(DIM)
        W2 = jax.random.normal(ks[7], (FF_INNER, DIM), dtype=jnp.float32) * s(FF_INNER)
        return {'x': x, 'media': media, 'media_mask': media_mask, 'ln_q_g': jnp.ones((DIM,), jnp.float32), 'ln_q_b': jnp.zeros((DIM,), jnp.float32), 'Wq': Wq, 'Wkv': Wkv, 'Wo': Wo, 'attn_gate': jax.random.normal(ks[8], (1,), jnp.float32) * 0.5, 'ln_ff_g': jnp.ones((DIM,), jnp.float32), 'ln_ff_b': jnp.zeros((DIM,), jnp.float32), 'W1': W1, 'W2': W2, 'ff_gate': jax.random.normal(ks[9], (1,), jnp.float32) * 0.5}
    _L3_xattn_all = _L3_xattn_setup()
    _L3_xattn_in = {k: v for k, v in _L3_xattn_all.items() if k in ('ln_q_g', 'ln_q_b', 'Wq', 'Wkv', 'Wo', 'attn_gate', 'ln_ff_g', 'ln_ff_b', 'W1', 'W2', 'ff_gate')}
    del _L3_xattn_all
    return {'x': x, 'ctx_1024': ctx_1024, 'pos_1xS': pos_1xS, 'mask_BxS2_bk0': mask_BxS2_bk0, 'mask_BxS_ik0': mask_BxS_ik0, 'L0_xattn_W_mem': _L0_xattn_in['W_mem'], 'L0_xattn_W_gate': _L0_xattn_in['W_gate'], 'L0_xattn_b_gate': _L0_xattn_in['b_gate'], 'L0_xattn_norm_w': _L0_xattn_in['norm_w'], 'L1_xattn_ln_q_g': _L1_xattn_in['ln_q_g'], 'L1_xattn_ln_q_b': _L1_xattn_in['ln_q_b'], 'L1_xattn_Wq': _L1_xattn_in['Wq'], 'L1_xattn_Wkv': _L1_xattn_in['Wkv'], 'L1_xattn_Wo': _L1_xattn_in['Wo'], 'L1_xattn_attn_gate': _L1_xattn_in['attn_gate'], 'L1_xattn_ln_ff_g': _L1_xattn_in['ln_ff_g'], 'L1_xattn_ln_ff_b': _L1_xattn_in['ln_ff_b'], 'L1_xattn_W1': _L1_xattn_in['W1'], 'L1_xattn_W2': _L1_xattn_in['W2'], 'L1_xattn_ff_gate': _L1_xattn_in['ff_gate'], 'L2_xattn_ln_in_w': _L2_xattn_in['ln_in_w'], 'L2_xattn_ln_post_attn_w': _L2_xattn_in['ln_post_attn_w'], 'L2_xattn_ln_post_cross_w': _L2_xattn_in['ln_post_cross_w'], 'L2_xattn_v_qkv': _L2_xattn_in['v_qkv'], 'L2_xattn_l_qkv': _L2_xattn_in['l_qkv'], 'L2_xattn_v_dense': _L2_xattn_in['v_dense'], 'L2_xattn_l_dense': _L2_xattn_in['l_dense'], 'L2_xattn_cq_w': _L2_xattn_in['cq_w'], 'L2_xattn_ckv_w': _L2_xattn_in['ckv_w'], 'L2_xattn_cdense_w': _L2_xattn_in['cdense_w'], 'L2_xattn_v_gate': _L2_xattn_in['v_gate'], 'L2_xattn_v_up': _L2_xattn_in['v_up'], 'L2_xattn_v_down': _L2_xattn_in['v_down'], 'L2_xattn_l_gate': _L2_xattn_in['l_gate'], 'L2_xattn_l_up': _L2_xattn_in['l_up'], 'L2_xattn_l_down': _L2_xattn_in['l_down'], 'L3_xattn_ln_q_g': _L3_xattn_in['ln_q_g'], 'L3_xattn_ln_q_b': _L3_xattn_in['ln_q_b'], 'L3_xattn_Wq': _L3_xattn_in['Wq'], 'L3_xattn_Wkv': _L3_xattn_in['Wkv'], 'L3_xattn_Wo': _L3_xattn_in['Wo'], 'L3_xattn_attn_gate': _L3_xattn_in['attn_gate'], 'L3_xattn_ln_ff_g': _L3_xattn_in['ln_ff_g'], 'L3_xattn_ln_ff_b': _L3_xattn_in['ln_ff_b'], 'L3_xattn_W1': _L3_xattn_in['W1'], 'L3_xattn_W2': _L3_xattn_in['W2'], 'L3_xattn_ff_gate': _L3_xattn_in['ff_gate']}

def reference(x, ctx_1024, pos_1xS, mask_BxS2_bk0, mask_BxS_ik0, L0_xattn_W_mem, L0_xattn_W_gate, L0_xattn_b_gate, L0_xattn_norm_w, L1_xattn_ln_q_g, L1_xattn_ln_q_b, L1_xattn_Wq, L1_xattn_Wkv, L1_xattn_Wo, L1_xattn_attn_gate, L1_xattn_ln_ff_g, L1_xattn_ln_ff_b, L1_xattn_W1, L1_xattn_W2, L1_xattn_ff_gate, L2_xattn_ln_in_w, L2_xattn_ln_post_attn_w, L2_xattn_ln_post_cross_w, L2_xattn_v_qkv, L2_xattn_l_qkv, L2_xattn_v_dense, L2_xattn_l_dense, L2_xattn_cq_w, L2_xattn_ckv_w, L2_xattn_cdense_w, L2_xattn_v_gate, L2_xattn_v_up, L2_xattn_v_down, L2_xattn_l_gate, L2_xattn_l_up, L2_xattn_l_down, L3_xattn_ln_q_g, L3_xattn_ln_q_b, L3_xattn_Wq, L3_xattn_Wkv, L3_xattn_Wo, L3_xattn_attn_gate, L3_xattn_ln_ff_g, L3_xattn_ln_ff_b, L3_xattn_W1, L3_xattn_W2, L3_xattn_ff_gate):
    import jax
    import jax.numpy as jnp

    def _L0_xattn_ref(hidden_states, memory, W_mem, W_gate, b_gate, norm_w):
        import jax, jax.numpy as jnp
        import numpy as np
        EPS = 1e-06

        def _rmsnorm(x, w):
            var = jnp.mean(jnp.square(x), axis=-1, keepdims=True)
            return x * jax.lax.rsqrt(var + EPS) * w
        D = hidden_states.shape[-1]
        memory_proj = jnp.einsum('bme,de->bmd', memory, W_mem)
        scores = jnp.einsum('bnd,bmd->bnm', hidden_states, memory_proj) / jnp.sqrt(jnp.float32(D))
        attn = jax.nn.softmax(scores, axis=-1)
        memory_context = jnp.einsum('bnm,bmd->bnd', attn, memory_proj)
        gate_input = jnp.concatenate([hidden_states, memory_context], axis=-1)
        gate = jax.nn.sigmoid(jnp.einsum('bnf,df->bnd', gate_input, W_gate) + b_gate)
        fused = hidden_states + gate * memory_context
        return _rmsnorm(fused, norm_w)

    def _L1_xattn_ref(x, media, media_mask, ln_q_g, ln_q_b, Wq, Wkv, Wo, attn_gate, ln_ff_g, ln_ff_b, W1, W2, ff_gate):
        import jax, jax.numpy as jnp
        import numpy as np
        DIM = 256
        DIM_MEDIA = 128
        HEADS = 16
        DIM_HEAD = 64
        INNER = HEADS * DIM_HEAD
        FF_INNER = 4 * DIM
        B, N_TOK, N_LAT = (4, 256, 64)
        EPS = 1e-05

        def layernorm(x, g, b):
            mu = jnp.mean(x, axis=-1, keepdims=True)
            var = jnp.var(x, axis=-1, keepdims=True)
            return (x - mu) * jax.lax.rsqrt(var + EPS) * g + b
        scale = DIM_HEAD ** (-0.5)
        qn = layernorm(x, ln_q_g, ln_q_b)
        q = qn @ Wq * scale
        kv = media @ Wkv
        k, v = jnp.split(kv, 2, axis=-1)
        split_heads = lambda t: t.reshape(t.shape[0], t.shape[1], HEADS, DIM_HEAD).transpose(0, 2, 1, 3)
        q, k, v = (split_heads(q), split_heads(k), split_heads(v))
        sim = jnp.einsum('bhid,bhjd->bhij', q, k)
        neg_inf = jnp.finfo(sim.dtype).min
        sim = jnp.where(media_mask[:, None, None, :], sim, neg_inf)
        attn = jax.nn.softmax(sim, axis=-1)
        out = jnp.einsum('bhij,bhjd->bhid', attn, v)
        out = out.transpose(0, 2, 1, 3).reshape(x.shape[0], x.shape[1], INNER)
        attn_out = out @ Wo
        x = x + jnp.tanh(attn_gate) * attn_out
        h = layernorm(x, ln_ff_g, ln_ff_b)
        h = jax.nn.gelu(h @ W1, approximate=False) @ W2
        x = x + jnp.tanh(ff_gate) * h
        return x

    def _L2_xattn_ref(hidden_states, encoder_outputs, token_type_ids, position_ids, ln_in_w, ln_post_attn_w, ln_post_cross_w, v_qkv, l_qkv, v_dense, l_dense, cq_w, ckv_w, cdense_w, v_gate, v_up, v_down, l_gate, l_up, l_down):
        import jax, jax.numpy as jnp
        import numpy as np
        H = 256
        NH = 16
        HD = H // NH
        CH = 128
        CC = 128
        CHD = CC // NH
        I = 688
        B = 2
        L = 256
        LE = 128
        EPS = 1e-06

        def rms_norm(x, w):
            xf = x.astype(jnp.float32)
            var = jnp.mean(xf * xf, axis=-1, keepdims=True)
            return (w * (xf * jax.lax.rsqrt(var + EPS))).astype(x.dtype)

        def expert_mask(tt):
            vm = jnp.zeros(tt.shape, dtype=bool)
            vm = vm.at[:, :-1].set((tt[:, :-1] == 1) & (tt[:, 1:] == 1))
            return vm

        def rotate_half(x):
            d = x.shape[-1] // 2
            return jnp.concatenate([-x[..., d:], x[..., :d]], axis=-1)

        def apply_rotary(q, k, position_ids, seq_len):
            inv = 1.0 / 10000.0 ** (jnp.arange(0, HD, 2, dtype=jnp.float32) / HD)
            t = jnp.arange(seq_len, dtype=jnp.float32)
            freqs = jnp.outer(t, inv)
            emb = jnp.concatenate([freqs, freqs], axis=-1)
            cos = jnp.cos(emb)[position_ids][:, None].astype(q.dtype)
            sin = jnp.sin(emb)[position_ids][:, None].astype(q.dtype)
            return (q * cos + rotate_half(q) * sin, k * cos + rotate_half(k) * sin)

        def sdpa(q, k, v, causal):
            scale = 1.0 / np.sqrt(q.shape[-1])
            scores = jnp.einsum('bhqd,bhkd->bhqk', q * scale, k)
            if causal:
                mask = jnp.tril(jnp.ones((q.shape[-2], k.shape[-2]), dtype=bool))
                scores = jnp.where(mask, scores, jnp.finfo(jnp.float32).min)
            p = jax.nn.softmax(scores.astype(jnp.float32), axis=-1).astype(q.dtype)
            return jnp.einsum('bhqk,bhkd->bhqd', p, v)

        def heads(x, nh, hd):
            b, l, _ = x.shape
            return x.reshape(b, l, nh, hd).transpose(0, 2, 1, 3)
        b, l, _ = hidden_states.shape
        vm = expert_mask(token_type_ids)[..., None]
        residual = hidden_states
        x = rms_norm(hidden_states, ln_in_w)
        mixed = jnp.where(vm, x @ v_qkv, x @ l_qkv)
        q, k, v = jnp.split(mixed, 3, axis=-1)
        q, k, v = (heads(q, NH, HD), heads(k, NH, HD), heads(v, NH, HD))
        q, k = apply_rotary(q, k, position_ids, l)
        ctx = sdpa(q, k, v, causal=True)
        ctx = ctx.transpose(0, 2, 1, 3).reshape(b, l, H)
        attn_out = jnp.where(vm, ctx @ v_dense, ctx @ l_dense)
        hidden_states = residual + attn_out
        ci = rms_norm(hidden_states, ln_post_cross_w)
        cq = heads(ci @ cq_w, NH, CHD)
        ckv = encoder_outputs @ ckv_w
        ck, cv = jnp.split(ckv, 2, axis=-1)
        ck, cv = (heads(ck, NH, CHD), heads(cv, NH, CHD))
        cctx = sdpa(cq, ck, cv, causal=False)
        cctx = cctx.transpose(0, 2, 1, 3).reshape(b, l, CC)
        hidden_states = hidden_states + cctx @ cdense_w
        mi = rms_norm(hidden_states, ln_post_attn_w)
        v_out = jax.nn.silu(mi @ v_gate) * (mi @ v_up) @ v_down
        l_out = jax.nn.silu(mi @ l_gate) * (mi @ l_up) @ l_down
        hidden_states = hidden_states + jnp.where(vm, v_out, l_out)
        return hidden_states

    def _L3_xattn_ref(x, media, media_mask, ln_q_g, ln_q_b, Wq, Wkv, Wo, attn_gate, ln_ff_g, ln_ff_b, W1, W2, ff_gate):
        import jax, jax.numpy as jnp
        import numpy as np
        DIM = 256
        DIM_MEDIA = 128
        HEADS = 16
        DIM_HEAD = 64
        INNER = HEADS * DIM_HEAD
        FF_INNER = 4 * DIM
        B, N_TOK, N_LAT = (4, 256, 64)
        EPS = 1e-05

        def layernorm(x, g, b):
            mu = jnp.mean(x, axis=-1, keepdims=True)
            var = jnp.var(x, axis=-1, keepdims=True)
            return (x - mu) * jax.lax.rsqrt(var + EPS) * g + b
        scale = DIM_HEAD ** (-0.5)
        qn = layernorm(x, ln_q_g, ln_q_b)
        q = qn @ Wq * scale
        kv = media @ Wkv
        k, v = jnp.split(kv, 2, axis=-1)
        split_heads = lambda t: t.reshape(t.shape[0], t.shape[1], HEADS, DIM_HEAD).transpose(0, 2, 1, 3)
        q, k, v = (split_heads(q), split_heads(k), split_heads(v))
        sim = jnp.einsum('bhid,bhjd->bhij', q, k)
        neg_inf = jnp.finfo(sim.dtype).min
        sim = jnp.where(media_mask[:, None, None, :], sim, neg_inf)
        attn = jax.nn.softmax(sim, axis=-1)
        out = jnp.einsum('bhij,bhjd->bhid', attn, v)
        out = out.transpose(0, 2, 1, 3).reshape(x.shape[0], x.shape[1], INNER)
        attn_out = out @ Wo
        x = x + jnp.tanh(attn_gate) * attn_out
        h = layernorm(x, ln_ff_g, ln_ff_b)
        h = jax.nn.gelu(h @ W1, approximate=False) @ W2
        x = x + jnp.tanh(ff_gate) * h
        return x
    x = _L0_xattn_ref(x, ctx_1024, L0_xattn_W_mem, L0_xattn_W_gate, L0_xattn_b_gate, L0_xattn_norm_w)
    x = _L1_xattn_ref(x, ctx_1024, mask_BxS2_bk0, L1_xattn_ln_q_g, L1_xattn_ln_q_b, L1_xattn_Wq, L1_xattn_Wkv, L1_xattn_Wo, L1_xattn_attn_gate, L1_xattn_ln_ff_g, L1_xattn_ln_ff_b, L1_xattn_W1, L1_xattn_W2, L1_xattn_ff_gate)
    x = _L2_xattn_ref(x, ctx_1024, mask_BxS_ik0, pos_1xS, L2_xattn_ln_in_w, L2_xattn_ln_post_attn_w, L2_xattn_ln_post_cross_w, L2_xattn_v_qkv, L2_xattn_l_qkv, L2_xattn_v_dense, L2_xattn_l_dense, L2_xattn_cq_w, L2_xattn_ckv_w, L2_xattn_cdense_w, L2_xattn_v_gate, L2_xattn_v_up, L2_xattn_v_down, L2_xattn_l_gate, L2_xattn_l_up, L2_xattn_l_down)
    x = _L3_xattn_ref(x, ctx_1024, mask_BxS2_bk0, L3_xattn_ln_q_g, L3_xattn_ln_q_b, L3_xattn_Wq, L3_xattn_Wkv, L3_xattn_Wo, L3_xattn_attn_gate, L3_xattn_ln_ff_g, L3_xattn_ln_ff_b, L3_xattn_W1, L3_xattn_W2, L3_xattn_ff_gate)
    return x

_drawn_inputs = setup_inputs


def setup_inputs(seed=0):
    import zlib

    import numpy as np

    out = dict(_drawn_inputs(seed))
    spreads = {'L0_xattn_norm_w': (1.0, 0.2),
     'L1_xattn_ln_q_g': (1.0, 0.6),
     'L1_xattn_ln_q_b': (0.0, 0.8),
     'L1_xattn_ln_ff_g': (1.0, 0.6),
     'L1_xattn_ln_ff_b': (0.0, 0.8),
     'L2_xattn_ln_in_w': (1.0, 0.6),
     'L2_xattn_ln_post_attn_w': (1.0, 0.6),
     'L2_xattn_ln_post_cross_w': (1.0, 0.6),
     'L3_xattn_ln_q_g': (1.0, 0.6),
     'L3_xattn_ln_q_b': (0.0, 2.0),
     'L3_xattn_ln_ff_g': (1.0, 0.6),
     'L3_xattn_ln_ff_b': (0.0, 2.0)}
    factors = {'L0_xattn_b_gate': 8.0,
     'L1_xattn_W1': 2.898,
     'L2_xattn_v_qkv': 8.0,
     'L2_xattn_v_dense': 6.666,
     'L2_xattn_cq_w': 64.0,
     'L2_xattn_v_gate': 7.124,
     'L2_xattn_v_up': 7.028,
     'L2_xattn_v_down': 7.138,
     'L3_xattn_W1': 15.376,
     'L2_xattn_l_dense': 8.0,
     'L2_xattn_ckv_w': 8.0,
     'L2_xattn_cdense_w': 7.952,
     'L2_xattn_l_gate': 8.0,
     'L2_xattn_l_up': 8.0,
     'L2_xattn_l_down': 8.0,
     'L3_xattn_Wq': 32.04,
     'L3_xattn_W2': 4.246,
     'L3_xattn_Wkv': 7.878,
     'L3_xattn_Wo': 7.768}
    for name, (base, spread) in spreads.items():
        noise = np.random.default_rng([zlib.crc32(name.encode()), seed]).standard_normal(out[name].shape)
        drawn = base * np.exp(spread * noise) if base else spread * noise
        out[name] = jnp.asarray(drawn.astype(out[name].dtype))
    for name, factor in factors.items():
        out[name] = (out[name] * factor).astype(out[name].dtype)
    return out
```

```python
from contextlib import ExitStack

import concourse.bass as bass
from concourse import mybir

F32 = mybir.dt.float32
BF16 = mybir.dt.bfloat16
I32 = mybir.dt.int32
U8 = mybir.dt.uint8
ALU = mybir.AluOpType
ACT = mybir.ActivationFunctionType
AX = mybir.AxisListType

P = 128
BATCH = 8
SLOTS = 2
ITERATIONS = BATCH // SLOTS
D = 256
DC = D // P
INNER = 1024
IC = INNER // P
FF = 688
FC = -(-FF // P)
FREST = FF - (FC - 1) * P
HEADS = 16
GROUP = 4
UNITS = HEADS // GROUP
HEAD = {"one": 64, "self": 16, "cross": 8, "three": 64}
MASKED = -(2.0 ** 127)
EPS = {"fuse": 1e-6, "one": 1e-5, "one_ff": 1e-5, "self": 1e-6, "cross": 1e-6, "mlp": 1e-6,
       "three": 1e-5, "three_ff": 1e-5}
NORMS = list(EPS)
FEATURES = ["one", "one_ff", "self", "cross", "mlp", "three", "three_ff"]
GATES = ["one", "one_ff", "three", "three_ff"]
PRODUCT_BANKS = {"mem": 1, "mcT": 1, "gate": 1, "kv": 4, "nT": 1, "q": 2, "qkv": 2, "qkT": 2, "cqk": 1,
                 "oT": 1, "wo": 1, "ff1": 2, "ff2": 1, "gu": 2 * FC // 2, "down": 1}
LINKS = {"mask": 2, "fuse": 5, "ln": 1, "rms": 2, "rms2": 4, "rinv": 1, "select": 1}


def steps():
    out = []

    def both(*names):
        for name in names:
            for s in range(SLOTS):
                out.append((*name, s) if isinstance(name, tuple) else (name, None, s))

    def attention(block, extra=None):
        units = [(s, u) for s in range(SLOTS) for u in range(UNITS)]
        for t in range(len(units) + 2):
            out.extend((extra or {}).get(t, []))
            if t < len(units):
                out.append(("scores", block, *units[t]))
            if t >= 2:
                out.append(("values", block, *units[t - 2]))
            if 1 <= t <= len(units):
                out.append(("turn", block, *units[t - 1]))

    both("mem")
    for kind in ("scores", "turn", "values"):
        for s in range(SLOTS):
            out.append((kind, "fuse", s, 0))
    both("mcT", "gate", ("kv", "one"))
    for s in range(SLOTS):
        out.extend([("nT", "one", s), ("q", "one", s)])
    after = {UNITS + 3: [("oT", "one", 0), ("wo", "one", 0)]}
    attention("one", after)
    out.extend([("nT", "one_ff", 0), ("ff1", "one", 0), ("oT", "one", 1), ("wo", "one", 1),
                ("ff2", "one", 0), ("nT", "one_ff", 1), ("ff1", "one", 1), ("ff2", "one", 1)])
    out.extend([("nT", "self", 0), ("qkv", "self", 0), ("nT", "self", 1), ("qkv", "self", 1)])
    both(("qkT", "self"))
    attention("self", {UNITS + 3: [("oT", "self", 0), ("wo", "self", 0)]})
    out.extend([("nT", "cross", 0), ("cqk", "cross", 0), ("oT", "self", 1), ("wo", "self", 1)])
    attention("cross", {3: [("nT", "cross", 1), ("cqk", "cross", 1)],
                        UNITS + 3: [("oT", "cross", 0), ("wo", "cross", 0)]})
    out.extend([("nT", "mlp", 0), ("oT", "cross", 1), ("wo", "cross", 1), ("gu", "mlp", 0), ("nT", "mlp", 1),
                ("gu", "mlp", 1), ("down", "mlp", 0), ("kv", "three", 0), ("down", "mlp", 1), ("kv", "three", 1)])
    for s in range(SLOTS):
        out.extend([("nT", "three", s), ("q", "three", s)])
    attention("three", {UNITS + 3: [("oT", "three", 0), ("wo", "three", 0)]})
    out.extend([("nT", "three_ff", 0), ("ff1", "three", 0), ("oT", "three", 1), ("wo", "three", 1),
                ("ff2", "three", 0), ("nT", "three_ff", 1), ("ff1", "three", 1), ("ff2", "three", 1)])
    return out


class Pool:

    def __init__(self, banks, full, emptied):
        self.banks, self.full, self.emptied = banks, full, emptied
        self.uses = [0] * len(banks)
        self.of = {}
        self.n = 0

    def plan(self, key):
        b = self.n % len(self.banks)
        self.of[key] = (b, self.uses[b])
        self.uses[b] += 1
        self.n += 1

    def bank(self, key):
        return self.banks[self.of[key][0]]

    def wait_before(self, eng, it, key):
        b, k = self.of[key]
        eng.wait_ge(self.emptied[b], it * self.uses[b] + k + 1)

    def wait_full(self, eng, it, key):
        b, k = self.of[key]
        eng.wait_ge(self.full[b], it * self.uses[b] + k + 2)

    def wait_full_before(self, eng, it, key):
        b, k = self.of[key]
        eng.wait_ge(self.full[b], it * self.uses[b] + k + 1)

    def wait_emptied(self, eng, it, key):
        b, k = self.of[key]
        eng.wait_ge(self.emptied[b], it * self.uses[b] + k + 2)

    def filled(self, ins, key):
        ins.then_inc(self.full[self.of[key][0]], 1)

    def empty(self, ins, key):
        ins.then_inc(self.emptied[self.of[key][0]], 1)


def build(nc, a, out):
    STEPS = steps()
    with ExitStack() as ctx:
        def sb(name, shape, dt=F32):
            return ctx.enter_context(nc.sbuf_tensor(name, shape, dt))

        def sem(name):
            return ctx.enter_context(nc.semaphore(name))

        w = {name: sb("w_" + name, shape) for name, shape in {
            "mem": [P, D], "gate": [P, 2 * DC, D],
            "one_q": [P, DC, INNER], "one_kv": [P, 2 * INNER], "one_o": [P, IC, D],
            "one_1": [P, DC, INNER], "one_2": [P, IC, D],
            "v_qkv": [P, DC, 3 * D], "l_qkv": [P, DC, 3 * D], "vl_dense": [P, DC, 2 * D],
            "cq": [P, DC, P], "ckv": [P, 2 * P], "cdense": [P, D],
            "v_gate": [P, DC, FC * P], "v_up": [P, DC, FC * P], "l_gate": [P, DC, FC * P], "l_up": [P, DC, FC * P],
            "v_down": [P, FC, D], "l_down": [P, FC, D],
            "three_q": [P, DC, INNER], "three_kv": [P, 2 * INNER], "three_o": [P, IC, D],
            "three_1": [P, DC, INNER], "three_2": [P, IC, D]}.items()}
        features = sb("features", [P, len(FEATURES), 2, DC])
        gates = sb("gates", [P, len(GATES)])
        tanh_gates = sb("tanh_gates", [P, len(GATES)])
        fuse_gain = sb("fuse_gain", [P, D])
        gate_bias = sb("gate_bias", [1, D])
        ones_row = sb("ones_row", [1, P])
        ones_row_bf = sb("ones_row_bf", [1, P], BF16)
        minus_half = sb("minus_half", [P, 1])
        ident = sb("ident", [P, P])
        ident_bf = sb("ident_bf", [P, P], BF16)
        member = sb("member", [P, 2 + 8 + 16])
        row_number = sb("row_number", [P, 1])
        causal = sb("causal", [P, P], BF16)
        rope = sb("rope", [P, 32])

        slots = range(SLOTS)
        x_in = [sb(f"x_in{s}", [P, D]) for s in slots]
        x_inT = [sb(f"x_inT{s}", [P, DC, P]) for s in slots]
        ctxT = [sb(f"ctxT{s}", [P, P]) for s in slots]
        keep_in = [sb(f"keep_in{s}", [1, P], U8) for s in slots]
        keep = [sb(f"keep{s}", [1, P], BF16) for s in slots]
        types = [sb(f"types{s}", [P, 2], I32) for s in slots]
        expert = [sb(f"expert{s}", [P, 4]) for s in slots]
        x = [sb(f"x{s}", [P, D]) for s in slots]
        xnT = [sb(f"xnT{s}", [P, DC, 2, P]) for s in slots]
        keys = [sb(f"keys{s}", [P, 2048]) for s in slots]
        queries = [sb(f"queries{s}", [P, INNER]) for s in slots]
        vals = [sb(f"vals{s}", [P, INNER]) for s in slots]
        heads = [sb(f"heads{s}", [P, INNER]) for s in slots]
        xn = [heads[s][:, 0:2 * D].rearrange("p (v d) -> p v d", v=2) for s in slots]
        context = [heads[s][:, 2 * D:3 * D] for s in slots]
        contextT = [queries[s][:, 0:DC * P].rearrange("p (c n) -> p c n", c=DC) for s in slots]
        memT = [keys[s][:, 0:DC * P].rearrange("p (c n) -> p c n", c=DC) for s in slots]
        mem = [keys[s][:, D:2 * D] for s in slots]
        gate_tanh = [queries[s][:, D:2 * D] for s in slots]
        gated = [queries[s][:, 2 * D:3 * D] for s in slots]
        hidden = [keys[s][:, 0:INNER].rearrange("p (c n) -> p c n", c=IC) for s in slots]
        hidden2 = [keys[s][:, 0:2 * FC * P].rearrange("p (e c n) -> p e c n", e=2, c=FC) for s in slots]
        roped = [keys[s][:, 0:2 * D] for s in slots]
        rope_a = [heads[s][:, 0:2 * D] for s in slots]
        rope_b = [heads[s][:, 2 * D:4 * D] for s in slots]
        silu = [[heads[s][:, D * b:D * b + D] for b in range(2)] for s in slots]
        probs = [sb(f"probs{i}", [P, GROUP, P]) for i in range(2)]
        probsT = [sb(f"probsT{i}", [P, GROUP, P]) for i in range(2)]

        causal_f = probs[0][:, 0, :]
        positions = probs[0][:, 1, :].bitcast(I32)
        tmp_pos = probs[0][:, 2:4, :]
        rope_rows = probs[1][:, 0, 0:32]

        def psum_pool(name, n):
            return Pool([ctx.enter_context(nc.psum_tensor(f"{name}{i}", [P, 512], F32)) for i in range(n)],
                        [sem(f"{name}_full{i}") for i in range(n)], [sem(f"{name}_emptied{i}") for i in range(n)])

        products, scores, turned, values = (psum_pool(n, 2) for n in ("products", "scores", "turned", "values"))

        unit_no = {}
        norm_no = {}
        gu_no = {}
        for kind, block, s, *u in STEPS:
            if kind == "scores":
                unit_no[block, s, u[0]] = len(unit_no)
                scores.plan((block, s, u[0]))
            elif kind == "turn":
                turned.plan((block, s, u[0]))
            elif kind == "values":
                values.plan((block, s, u[0]))
            else:
                n = IC // 4 if kind == "oT" and HEAD[block] == 64 else PRODUCT_BANKS[kind]
                for i in range(n):
                    products.plan((kind, block, s, i))
                    if kind == "gu":
                        gu_no[s, i] = len(gu_no)
            for name in {"gate": ["fuse", "one"], "wo": {"one": ["one_ff"], "self": ["cross"], "cross": ["mlp"],
                                                          "three": ["three_ff"]}.get(block, []),
                         "ff2": ["self"] if block == "one" else [], "down": ["three"]}.get(kind, []):
                norm_no[name, s] = len(norm_no)
        N_UNITS, N_NORMS = len(unit_no), len(norm_no)
        xn_no = {key: n for n, key in enumerate(k for k in norm_no if k[0] != "fuse")}
        N_LINKS = 0
        for kind, block, s, *u in STEPS:
            N_LINKS += {"mem": LINKS["mask"], "values": LINKS["rinv"], "gate": LINKS["fuse"] + LINKS["ln"],
                        "wo": {"one": LINKS["ln"], "three": LINKS["ln"], "self": LINKS["select"] + LINKS["rms"],
                               "cross": LINKS["rms"]}.get(block, 0),
                        "ff2": LINKS["rms2"] if block == "one" else 0,
                        "down": LINKS["select"] + LINKS["ln"]}.get(kind, 0)

        moments = sb("moments", [P, N_NORMS, 6])
        mean_var = sb("mean_var", [P, N_NORMS, 2])
        square = sb("square", [P, N_NORMS])
        var_eps = sb("var_eps", [P, N_NORMS])
        rstd = sb("rstd", [P, N_NORMS])
        rstd_expert = sb("rstd_expert", [P, SLOTS, 2])
        minus_max = sb("minus_max", [P, N_UNITS, GROUP])
        total = sb("total", [P, N_UNITS, GROUP])
        inv_total = sb("inv_total", [P, N_UNITS, GROUP])

        s_weights = {g: sem("weights_loaded_" + g) for g in ("fuse", "one_kv", "one", "one_ff", "two_a", "two_mlp", "three")}
        n_weights = dict.fromkeys(s_weights, 0)
        s_pads = sem("weight_pads_zeroed")
        s_consts = sem("constants_loaded")
        s_set = sem("constants_set")
        s_onehot = sem("positions_one_hot")
        s_rope_full = sem("rope_rows_gathered")
        s_rope = sem("rope_ready")
        s_tanh_gates = sem("tanh_gates_ready")
        s_x = [sem(f"x_loaded{s}") for s in slots]
        s_side = [sem(f"side_inputs_loaded{s}") for s in slots]
        s_x_used = [sem(f"x_input_used{s}") for s in slots]
        s_side_used = [sem(f"side_inputs_used{s}") for s in slots]
        s_keep = sem("key_masks_ready")
        s_link = sem("vector_done")
        s_var = sem("variance_ready")
        s_rstd = sem("rstd_ready")
        s_xn = sem("normalised_ready")
        s_max = sem("minus_max_ready")
        s_roped = sem("roped_ready")
        s_silu = sem("silu_ready")
        s_stored = [sem(f"result_stored{s}") for s in slots]
        s_x_free = [sem(f"x_free{s}") for s in slots]

        block_ = ctx.enter_context(nc.Block())

        WEIGHTS = [("fuse", "mem"), ("fuse", "gate"), ("one_kv", "one_kv"), ("one", "one_q"), ("one", "one_o"),
                   ("one_ff", "one_1"), ("one_ff", "one_2"), ("two_a", "v_qkv"), ("two_a", "l_qkv"),
                   ("two_a", "vl_dense"), ("two_a", "cq"), ("two_a", "ckv"), ("two_a", "cdense"),
                   ("two_mlp", "v_gate"), ("two_mlp", "v_up"), ("two_mlp", "l_gate"), ("two_mlp", "l_up"),
                   ("two_mlp", "v_down"), ("two_mlp", "l_down"), ("three", "three_kv"), ("three", "three_q"),
                   ("three", "three_o"), ("three", "three_1"), ("three", "three_2")]
        for group, name in WEIGHTS:
            n_weights[group] += 32 if name.endswith("_down") else 16
        CONSTS = [(features[:], a["features"]), (gates[:], a["gates"].partition_broadcast(P)),
                  (fuse_gain[:], a["fuse_gain"].partition_broadcast(P)), (gate_bias[:], a["gate_bias"]),
                  (ident[:], a["ident"]), (causal_f, a["causal"]), (member[:], a["member"]),
                  (row_number[:], a["row_number"]), (rope_rows, a["rope_rows"]),
                  (positions, a["positions"].partition_broadcast(P))]

        def load_weight(sp, group, name):
            if name.endswith("_down"):
                sp.dma_start(w[name][:, 0:FC - 1, :], a[name][0]).then_inc(s_weights[group], 16)
                sp.dma_start(w[name][0:FREST, FC - 1, :], a[name][1]).then_inc(s_weights[group], 16)
            elif name.endswith("_gate") or name.endswith("_up"):
                sp.dma_start(w[name][:, :, 0:FF], a[name]).then_inc(s_weights[group], 16)
            else:
                sp.dma_start(w[name][:], a[name]).then_inc(s_weights[group], 16)

        def made_by(name):
            return {"fuse": ("gate", None), "one": ("gate", None), "one_ff": ("wo", "one"), "self": ("ff2", "one"),
                    "cross": ("wo", "self"), "mlp": ("wo", "cross"), "three": ("down", "mlp"),
                    "three_ff": ("wo", "three")}[name]

        @block_.sync
        def _(sp):
            for group, name in WEIGHTS[:2]:
                load_weight(sp, group, name)

            def load_x(it, s):
                sp.wait_ge(s_x_used[s], it + 1)
                b = it * SLOTS + s
                sp.dma_start(x_in[s][:], a["x"][bass.ds(b, 1), :, :].rearrange("o p n -> p (o n)")).then_inc(s_x[s], 16)
                sp.dma_start(x_inT[s][:], a["xT"][bass.ds(b, 1), :, :, :].rearrange("o p c n -> p (o c) n")).then_inc(s_x[s], 16)

            def load_side(it, s):
                sp.wait_ge(s_side_used[s], it + 1)
                b = it * SLOTS + s
                sp.dma_start(ctxT[s][:], a["ctxT"][bass.ds(b, 1), :, :].rearrange("o p n -> p (o n)")).then_inc(s_side[s], 16)
                sp.dma_start(keep_in[s][:], a["keep"][bass.ds(b, 1), :]).then_inc(s_side[s], 16)
                sp.dma_start(types[s][:], a["types"][bass.ds(b, 1), :, :].rearrange("o p n -> p (o n)")).then_inc(s_side[s], 16)

            with sp.Fori(0, ITERATIONS) as it:
                for s in slots:
                    load_x(it, s)
                for s in slots:
                    load_side(it, s)

        @block_.gpsimd
        def _(pool):
            for p in (products, scores, turned, values):
                for q in (*p.full, *p.emptied):
                    pool.sem_inc(q, 1)
            for q in (*s_x_used, *s_side_used, *s_x_free):
                pool.sem_inc(q, 1)
            nc.gpsimd.memset(minus_half[:], -0.5).then_inc(s_set, 1)
            pool.wait_ge(s_set, 1)
            with pool.Fori(0, ITERATIONS) as it:
                done = 0
                for kind, block, s, *_u in STEPS:
                    names = [k for k in NORMS if (k, s) in norm_no and made_by(k) == (kind, block)]
                    for name in names:
                        n = norm_no[name, s]
                        assert n == done
                        done += 1
                        pool.wait_ge(s_var, it * N_NORMS + n + 1)
                        nc.gpsimd.tensor_tensor(rstd[:, n:n + 1], var_eps[:, n:n + 1], minus_half[:],
                                                ALU.pow).then_inc(s_rstd, 1)
                    if kind == "ff2" and block == "three":
                        pool.wait_ge(s_set, 1)
                        products.wait_emptied(pool, it, (kind, block, s, 0))
                        b = it * SLOTS + s
                        pool.dma_start(out[bass.ds(b, 1), :, :].rearrange("o p n -> p (o n)"), x[s][:]).then_inc(s_stored[s], 16)
                        pool.wait_ge(s_stored[s], (it + 1) * 16)
                        pool.sem_inc(s_x_free[s], 1)

        @block_.tensor
        def _(pe):
            mm = nc.tensor.matmul

            def have(group):
                pe.wait_ge(s_weights[group], n_weights[group])

            pe.wait_ge(s_onehot, 1)
            mm(values.banks[0][:, 0:32], tmp_pos[:, 1, :], rope_rows, start=True, stop=True).then_inc(s_rope_full, 1)
            pe.wait_ge(s_rope, 1)
            pe.wait_ge(s_pads, 6)

            with pe.Fori(0, ITERATIONS) as it:
                def fill(kind, block, s, i):
                    key = (kind, block, s, i)
                    products.wait_before(pe, it, key)
                    return key, products.bank(key)

                for kind, block, s, *u in STEPS:
                    if kind == "mem":
                        pe.wait_ge(s_side[s], (it + 1) * 48)
                        have("fuse")
                        key, bank = fill(kind, block, s, 0)
                        for c in range(DC):
                            mm(bank[:, c * P:(c + 1) * P], w["mem"][:, c * P:(c + 1) * P], ctxT[s][:], start=True, stop=True)
                        products.filled(mm(bank[:, D:2 * D], ctxT[s][:], w["mem"][:], start=True, stop=True), key)

                    elif kind == "scores":
                        key = (block, s, u[0])
                        scores.wait_before(pe, it, key)
                        bank = scores.bank(key)
                        q0 = u[0]
                        if block == "fuse":
                            pe.wait_ge(s_x[s], (it + 1) * 32)
                            products.wait_emptied(pe, it, ("mem", None, s, 0))
                            for c in range(DC):
                                last = mm(bank[:, 0:P], x_inT[s][:, c, :], memT[s][:, c, :], start=(c == 0), stop=(c == DC - 1))
                        elif block == "self":
                            if q0 == 0:
                                for i in range(2):
                                    products.wait_emptied(pe, it, ("qkT", block, s, i))
                            mm(bank[:], ident_bf[:], causal[:].unsqueeze(1).to_broadcast([P, GROUP, P]), start=True, stop=False)
                            t = q0 // 2
                            last = mm(bank[:], queries[s][:, t * P:(t + 1) * P],
                                      keys[s][:, q0 * 512:(q0 + 1) * 512], start=False, stop=True)
                        elif block == "cross":
                            if q0 == 0:
                                products.wait_emptied(pe, it, ("cqk", block, s, 0))
                            last = mm(bank[:], queries[s][:, 0:P], keys[s][:, q0 * 512:(q0 + 1) * 512], start=True, stop=True)
                        else:
                            if q0 == 0:
                                products.wait_emptied(pe, it, ("q", block, s, 1))
                                pe.wait_ge(s_keep, it * SLOTS + s + 1)
                            mm(bank[:], ones_row_bf[:], keep[s][:].unsqueeze(1).to_broadcast([1, GROUP, P]), start=True, stop=False)
                            for j in range(2):
                                t = 2 * q0 + j
                                last = mm(bank[:, j * 256:(j + 1) * 256], queries[s][:, t * P:(t + 1) * P],
                                          keys[s][:, t * 256:(t + 1) * 256], start=False, stop=(j == 1))
                        scores.filled(last, key)

                    elif kind == "turn":
                        key = (block, s, u[0])
                        turned.wait_before(pe, it, key)
                        scores.wait_emptied(pe, it, key)
                        b = turned.of[key][0]
                        for j in range(1 if block == "fuse" else GROUP):
                            last = nc.tensor.transpose(turned.bank(key)[:, j * P:(j + 1) * P], probs[b][:, j, :], ident[:])
                        turned.filled(last, key)

                    elif kind == "values":
                        key = (block, s, u[0])
                        values.wait_before(pe, it, key)
                        turned.wait_emptied(pe, it, key)
                        b = turned.of[key][0]
                        bank = values.bank(key)
                        if block == "fuse":
                            last = mm(bank[:, 0:D], probsT[b][:, 0, :], mem[s], start=True, stop=True)
                        else:
                            h = HEAD[block]
                            for j in range(GROUP):
                                c = (u[0] * GROUP + j) * h
                                last = mm(bank[:, j * h:(j + 1) * h], probsT[b][:, j, :], vals[s][:, c:c + h], start=True, stop=True)
                                if block == "three" and u[0] == UNITS - 1 and j == 0:
                                    last.then_inc(s_side_used[s], 1)
                        values.filled(last, key)

                    elif kind == "mcT":
                        key, bank = fill(kind, block, s, 0)
                        values.wait_emptied(pe, it, ("fuse", s, 0))
                        for c in range(DC):
                            last = nc.tensor.transpose(bank[:, c * P:(c + 1) * P], context[s][:, c * P:(c + 1) * P], ident[:])
                        products.filled(last, key)

                    elif kind == "gate":
                        key, bank = fill(kind, block, s, 0)
                        products.wait_emptied(pe, it, ("mcT", block, s, 0))
                        mm(bank[:, 0:D], ones_row[:], gate_bias[:], start=True, stop=False)
                        for c in range(2 * DC):
                            lhs = x_inT[s][:, c, :] if c < DC else contextT[s][:, c - DC, :]
                            last = mm(bank[:, 0:D], lhs, w["gate"][:, c, :], start=False, stop=(c == 2 * DC - 1))
                        products.filled(last, key)

                    elif kind == "kv":
                        wkv = w[block + "_kv"]
                        have("one_kv" if block == "one" else "three")
                        for i in range(4):
                            key, bank = fill(kind, block, s, i)
                            if i % 2 == 0:
                                for j in range(4):
                                    t = 2 * i + j
                                    last = mm(bank[:, j * P:(j + 1) * P], wkv[:, t * P:(t + 1) * P], ctxT[s][:], start=True, stop=True)
                            else:
                                c = INNER + (i // 2) * 512
                                last = mm(bank[:], ctxT[s][:], wkv[:, c:c + 512], start=True, stop=True)
                            products.filled(last, key)

                    elif kind == "nT":
                        key, bank = fill(kind, block, s, 0)
                        pe.wait_ge(s_xn, it * len(xn_no) + xn_no[block, s] + 1)
                        nv = 2 if block == "self" else 1
                        for c in range(DC):
                            for v in range(nv):
                                last = nc.tensor.transpose(bank[:, (c * nv + v) * P:(c * nv + v + 1) * P],
                                                           xn[s][:, v, c * P:(c + 1) * P], ident[:])
                                if block == "one" and c == 0:
                                    last.then_inc(s_x_used[s], 1)
                        products.filled(last, key)

                    elif kind in ("q", "ff1"):
                        name = block + ("_q" if kind == "q" else "_1")
                        have({"one_q": "one", "one_1": "one_ff"}.get(name, "three"))
                        products.wait_emptied(pe, it, ("nT", block + ("_ff" if kind == "ff1" else ""), s, 0))
                        for i in range(2):
                            key, bank = fill(kind, block, s, i)
                            for j in range(4):
                                t = 4 * i + j
                                for c in range(DC):
                                    last = mm(bank[:, j * P:(j + 1) * P], w[name][:, c, t * P:(t + 1) * P], xnT[s][:, c, 0, :],
                                              start=(c == 0), stop=(c == DC - 1))
                            products.filled(last, key)

                    elif kind == "qkv":
                        have("two_a")
                        products.wait_emptied(pe, it, ("nT", block, s, 0))
                        for i, (c0, n) in enumerate(((0, 512), (512, 256))):
                            key, bank = fill(kind, block, s, i)
                            k = 0
                            for v, name in enumerate(("v_qkv", "l_qkv")):
                                for c in range(DC):
                                    last = mm(bank[:, 0:n], xnT[s][:, c, v, :], w[name][:, c, c0:c0 + n], start=(k == 0), stop=(k == 3))
                                    k += 1
                            products.filled(last, key)

                    elif kind == "qkT":
                        for i in range(2):
                            key, bank = fill(kind, block, s, i)
                            pe.wait_ge(s_roped, it * SLOTS + s + 1)
                            for c in range(DC):
                                last = nc.tensor.transpose(bank[:, c * P:(c + 1) * P], roped[s][:, (i * DC + c) * P:(i * DC + c + 1) * P], ident[:])
                            products.filled(last, key)

                    elif kind == "cqk":
                        key, bank = fill(kind, block, s, 0)
                        mm(bank[:, P:2 * P], w["ckv"][:, 0:P], ctxT[s][:], start=True, stop=True)
                        mm(bank[:, 2 * P:3 * P], ctxT[s][:], w["ckv"][:, P:2 * P], start=True, stop=True)
                        products.wait_emptied(pe, it, ("nT", block, s, 0))
                        for c in range(DC):
                            last = mm(bank[:, 0:P], w["cq"][:, c, :], xnT[s][:, c, 0, :], start=(c == 0), stop=(c == DC - 1))
                        products.filled(last, key)

                    elif kind == "oT":
                        n = HEAD[block] * HEADS // P
                        values.wait_emptied(pe, it, (block, s, UNITS - 1))
                        for i in range(-(-n // 4)):
                            key, bank = fill(kind, block, s, i)
                            for j in range(min(4, n)):
                                t = 4 * i + j
                                last = nc.tensor.transpose(bank[:, j * P:(j + 1) * P], heads[s][:, t * P:(t + 1) * P], ident[:])
                            products.filled(last, key)

                    elif kind in ("wo", "ff2"):
                        key, bank = fill(kind, block, s, 0)
                        if kind == "wo":
                            n = HEAD[block] * HEADS // P
                            have({"one": "one", "three": "three"}.get(block, "two_a"))
                            products.wait_emptied(pe, it, ("oT", block, s, -(-n // 4) - 1))
                            weight = {"self": w["vl_dense"], "cross": w["cdense"][:].unsqueeze(1)}.get(block)
                            weight = w[block + "_o"] if weight is None else weight
                            lhs = [queries[s][:, t * P:(t + 1) * P] for t in range(n)]
                        else:
                            n = IC
                            have({"one": "one_ff"}.get(block, "three"))
                            products.wait_emptied(pe, it, ("ff1", block, s, 1))
                            weight = w[block + "_2"]
                            lhs = [hidden[s][:, t, :] for t in range(n)]
                        width = 2 * D if block == "self" else D
                        for t in range(n):
                            last = mm(bank[:, 0:width], lhs[t], weight[:, t, :], start=(t == 0), stop=(t == n - 1))
                        products.filled(last, key)

                    elif kind == "gu":
                        have("two_mlp")
                        products.wait_emptied(pe, it, ("nT", block, s, 0))
                        for i in range(2 * FC // 2):
                            key, bank = fill(kind, block, s, i)
                            e, pair = "vl"[i // (FC // 2)], i % (FC // 2)
                            for g, name in enumerate(("_gate", "_up")):
                                for j in range(2):
                                    t = 2 * pair + j
                                    for c in range(DC):
                                        last = mm(bank[:, (2 * g + j) * P:(2 * g + j + 1) * P], w[e + name][:, c, t * P:(t + 1) * P],
                                                  xnT[s][:, c, 0, :], start=(c == 0), stop=(c == DC - 1))
                            products.filled(last, key)

                    elif kind == "down":
                        key, bank = fill(kind, block, s, 0)
                        products.wait_emptied(pe, it, ("gu", block, s, 2 * FC // 2 - 1))
                        for e, name in enumerate(("v_down", "l_down")):
                            for t in range(FC):
                                last = mm(bank[:, e * D:(e + 1) * D], hidden2[s][:, e, t, :], w[name][:, t, :], start=(t == 0), stop=(t == FC - 1))
                        products.filled(last, key)

        @block_.scalar
        def _(act):
            for group, name in WEIGHTS[2:5]:
                load_weight(act, group, name)
            for dst, src in CONSTS:
                act.dma_start(dst, src).then_inc(s_consts, 16)
            act.wait_ge(s_pads, 6)
            for group, name in WEIGHTS[5:]:
                load_weight(act, group, name)
            act.wait_ge(s_consts, 16 * len(CONSTS))
            nc.scalar.activation(tanh_gates[:], gates[:], ACT.Tanh).then_inc(s_tanh_gates, 1)

            with act.Fori(0, ITERATIONS) as it:
                for kind, block, s, *u in STEPS:
                    if kind == "mem":
                        key = (kind, block, s, 0)
                        products.wait_full(act, it, key)
                        bank = products.bank(key)
                        nc.scalar.activation(memT[s], bank[:, 0:D].rearrange("p (c n) -> p c n", c=DC), ACT.Copy, scale=D ** -0.5)
                        products.empty(nc.scalar.activation(mem[s], bank[:, D:2 * D], ACT.Copy), key)

                    elif kind == "scores":
                        key = (block, s, u[0])
                        n = unit_no[key]
                        act.wait_ge(s_max, it * N_UNITS + n + 1)
                        turned.wait_full_before(act, it, key)
                        b = turned.of[key][0]
                        for j in range(1 if block == "fuse" else GROUP):
                            last = nc.scalar.activation(probs[b][:, j, :], scores.bank(key)[:, j * P:(j + 1) * P], ACT.Exp,
                                                        bias=minus_max[:, n, j:j + 1], accum_out=total[:, n, j:j + 1])
                        scores.empty(last, key)

                    elif kind == "mcT":
                        key = (kind, block, s, 0)
                        products.wait_full(act, it, key)
                        products.empty(nc.scalar.activation(contextT[s], products.bank(key)[:, 0:D].rearrange("p (c n) -> p c n", c=DC),
                                                            ACT.Copy), key)

                    elif kind == "gate":
                        key = (kind, block, s, 0)
                        products.wait_full(act, it, key)
                        products.empty(nc.scalar.activation(gate_tanh[s], products.bank(key)[:, 0:D], ACT.Tanh, scale=0.5), key)

                    elif kind == "kv":
                        for i in (1, 3):
                            key = (kind, block, s, i)
                            products.wait_full(act, it, key)
                            products.empty(nc.scalar.activation(vals[s][:, (i // 2) * 512:(i // 2 + 1) * 512], products.bank(key)[:], ACT.Copy), key)

                    elif kind == "nT":
                        key = (kind, block, s, 0)
                        products.wait_full(act, it, key)
                        nv = 2 if block == "self" else 1
                        f = FEATURES.index(block)
                        for c in range(DC):
                            src = products.bank(key)[:, c * nv * P:(c + 1) * nv * P].rearrange("p (v n) -> p v n", v=nv)
                            if block in ("self", "cross", "mlp"):
                                last = nc.scalar.activation(xnT[s][:, c, 0:nv, :], src, ACT.Copy, scale=features[:, f, 0, c:c + 1])
                            else:
                                last = nc.scalar.activation(xnT[s][:, c, 0:nv, :], src, ACT.Identity, scale=features[:, f, 0, c:c + 1],
                                                            bias=features[:, f, 1, c:c + 1])
                        products.empty(last, key)

                    elif kind == "q":
                        for i in range(2):
                            key = (kind, block, s, i)
                            products.wait_full(act, it, key)
                            products.empty(nc.scalar.activation(queries[s][:, i * 512:(i + 1) * 512], products.bank(key)[:], ACT.Copy,
                                                                scale=HEAD[block] ** -0.5), key)

                    elif kind == "qkT":
                        key = (kind, block, s, 0)
                        products.wait_full(act, it, key)
                        products.empty(nc.scalar.activation(queries[s][:, 0:D], products.bank(key)[:, 0:D], ACT.Copy,
                                                            scale=HEAD[block] ** -0.5), key)

                    elif kind == "oT":
                        n = HEAD[block] * HEADS // P
                        for i in range(-(-n // 4)):
                            key = (kind, block, s, i)
                            m = min(n, 4) * P
                            products.wait_full(act, it, key)
                            products.empty(nc.scalar.activation(queries[s][:, i * 512:i * 512 + m], products.bank(key)[:, 0:m], ACT.Copy), key)

                    elif kind == "ff1":
                        for i in range(2):
                            key = (kind, block, s, i)
                            products.wait_full(act, it, key)
                            products.empty(nc.scalar.activation(hidden[s][:, 4 * i:4 * i + 4, :], products.bank(key)[:].rearrange("p (c n) -> p c n", c=4),
                                                                ACT.Gelu), key)

                    elif kind == "gu":
                        for i in range(2 * FC // 2):
                            key = (kind, block, s, i)
                            products.wait_full(act, it, key)
                            nc.scalar.activation(silu[s][i % 2], products.bank(key)[:, 0:D], ACT.Silu).then_inc(s_silu, 1)

        @block_.vector
        def _(dve):
            state = {"n": 0, "it": 0}

            def link(ins):
                state["n"] += 1
                ins.then_inc(s_link, 1)
                dve.wait_ge(s_link, state["it"] * N_LINKS + SETUP_LINKS + state["n"])

            SETUP_LINKS = 4
            for e in "vl":
                nc.vector.memset(w[e + "_gate"][:, :, FF:FC * P], 0.0).then_inc(s_pads, 1)
                nc.vector.memset(w[e + "_up"][:, :, FF:FC * P], 0.0).then_inc(s_pads, 1)
                nc.vector.memset(w[e + "_down"][:, FC - 1, :], 0.0).then_inc(s_pads, 1)
            nc.vector.memset(ones_row[:], 1.0)
            nc.vector.memset(ones_row_bf[:], 1.0)
            dve.wait_ge(s_consts, 16 * len(CONSTS))
            nc.vector.tensor_copy(ident_bf[:], ident[:])
            nc.vector.tensor_copy(causal[:], causal_f)

            def setup_link(ins, n):
                ins.then_inc(s_link, 1)
                dve.wait_ge(s_link, n)

            setup_link(nc.vector.tensor_scalar(tmp_pos[:, 1, :], positions, 0.0, float(P), ALU.is_lt, ALU.mult), 1)
            setup_link(nc.vector.tensor_tensor(tmp_pos[:, 0, :], positions, tmp_pos[:, 1, :], ALU.add), 2)
            setup_link(nc.vector.tensor_scalar(tmp_pos[:, 1, :], tmp_pos[:, 0, :], 0.0, float(P - 1), ALU.max, ALU.min), 3)
            setup_link(nc.vector.tensor_scalar(tmp_pos[:, 0, :], tmp_pos[:, 1, :], row_number[:, 0:1], None, ALU.is_equal), 4)
            nc.vector.tensor_copy(tmp_pos[:, 1, :], tmp_pos[:, 0, :]).then_inc(s_onehot, 1)
            dve.wait_ge(s_rope_full, 1)
            nc.vector.tensor_copy(rope[:], values.banks[0][:, 0:32]).then_inc(s_rope, 1)
            dve.wait_ge(s_rope, 1)
            dve.wait_ge(s_set, 1)
            dve.wait_ge(s_tanh_gates, 1)

            with dve.Fori(0, ITERATIONS) as it:
                state["it"] = it
                state["n"] = 0

                def norm(name, s):
                    n = norm_no[name, s]
                    nc.vector.bn_stats(moments[:, n, :], x[s][:])
                    dve.drain()
                    link(nc.vector.bn_aggr(mean_var[:, n, :], moments[:, n, :]))
                    mean, var = mean_var[:, n, 0:1], mean_var[:, n, 1:2]
                    centred = name in ("one", "one_ff", "three", "three_ff")
                    if not centred:
                        link(nc.vector.scalar_tensor_tensor(out=square[:, n:n + 1], in0=mean, scalar=mean, in1=var, op0=ALU.mult, op1=ALU.add))
                        var = square[:, n:n + 1]
                    nc.vector.tensor_scalar(var_eps[:, n:n + 1], var, EPS[name], None, ALU.add).then_inc(s_var, 1)
                    dve.wait_ge(s_rstd, it * N_NORMS + n + 1)
                    r = rstd[:, n:n + 1]
                    if name == "fuse":
                        link(nc.vector.scalar_tensor_tensor(out=x[s][:], in0=x[s][:], scalar=r, in1=fuse_gain[:], op0=ALU.mult, op1=ALU.mult))
                    elif name == "self":
                        for v in range(2):
                            link(nc.vector.tensor_scalar(rstd_expert[:, s, v:v + 1], r, expert[s][:, v:v + 1], None, ALU.mult))
                        nc.vector.tensor_scalar(xn[s][:, 0, :], x[s][:], rstd_expert[:, s, 0:1], None, ALU.mult)
                        nc.vector.tensor_scalar(xn[s][:, 1, :], x[s][:], rstd_expert[:, s, 1:2], None, ALU.mult).then_inc(s_xn, 1)
                    elif centred:
                        nc.vector.tensor_scalar(xn[s][:, 0, :], x[s][:], mean, r, ALU.subtract, ALU.mult).then_inc(s_xn, 1)
                    else:
                        nc.vector.tensor_scalar(xn[s][:, 0, :], x[s][:], r, None, ALU.mult).then_inc(s_xn, 1)

                for kind, block, s, *u in STEPS:
                    if kind == "mem":
                        dve.wait_ge(s_side[s], (it + 1) * 48)
                        nc.vector.tensor_scalar(keep[s][:], keep_in[s][:], 1.0, -MASKED, ALU.subtract, ALU.mult).then_inc(s_keep, 1)
                        link(nc.vector.tensor_scalar(expert[s][:, 2:4], types[s][:], 1.0, None, ALU.is_equal))
                        link(nc.vector.tensor_tensor(expert[s][:, 0:1], expert[s][:, 2:3], expert[s][:, 3:4], ALU.mult))
                        nc.vector.tensor_scalar(expert[s][:, 1:2], expert[s][:, 0:1], -1.0, 1.0, ALU.mult, ALU.add)

                    elif kind == "scores":
                        key = (block, s, u[0])
                        n = unit_no[key]
                        g = 1 if block == "fuse" else GROUP
                        scores.wait_full(dve, it, key)
                        nc.vector.tensor_reduce(minus_max[:, n, 0:g], scores.bank(key)[:, 0:g * P].rearrange("p (h k) -> p h k", h=g),
                                                AX.X, ALU.max, negate=True).then_inc(s_max, 1)

                    elif kind == "turn":
                        key = (block, s, u[0])
                        g = 1 if block == "fuse" else GROUP
                        turned.wait_full(dve, it, key)
                        values.wait_full_before(dve, it, key)
                        b = turned.of[key][0]
                        turned.empty(nc.vector.tensor_copy(probsT[b][:, 0:g, :], turned.bank(key)[:, 0:g * P].rearrange("p (h k) -> p h k", h=g)), key)

                    elif kind == "values":
                        key = (block, s, u[0])
                        n = unit_no[key]
                        g = 1 if block == "fuse" else GROUP
                        values.wait_full(dve, it, key)
                        link(nc.vector.reciprocal(inv_total[:, n, 0:g], total[:, n, 0:g]))
                        if block == "fuse":
                            ins = nc.vector.tensor_scalar(context[s], values.bank(key)[:, 0:D], inv_total[:, n, 0:1], None, ALU.mult)
                        else:
                            h = HEAD[block]
                            c = u[0] * GROUP * h
                            ins = nc.vector.tensor_tensor(heads[s][:, c:c + GROUP * h].rearrange("p (g h) -> p g h", g=GROUP),
                                                          values.bank(key)[:, 0:GROUP * h].rearrange("p (g h) -> p g h", g=GROUP),
                                                          inv_total[:, n, :].unsqueeze(2).to_broadcast([P, GROUP, h]), ALU.mult)
                        values.empty(ins, key)

                    elif kind == "gate":
                        products.wait_emptied(dve, it, (kind, block, s, 0))
                        link(nc.vector.scalar_tensor_tensor(out=gated[s], in0=gate_tanh[s], scalar=1.0, in1=context[s], op0=ALU.add, op1=ALU.mult))
                        dve.wait_ge(s_x_free[s], it + 1)
                        link(nc.vector.scalar_tensor_tensor(out=x[s][:], in0=gated[s], scalar=0.5, in1=x_in[s][:], op0=ALU.mult, op1=ALU.add))
                        norm("fuse", s)
                        norm("one", s)

                    elif kind == "kv":
                        for i in (0, 2):
                            key = (kind, block, s, i)
                            products.wait_full(dve, it, key)
                            products.empty(nc.vector.tensor_tensor(
                                keys[s][:, i * 512:(i + 2) * 512].rearrange("p (c h n) -> p c h n", c=4, h=2),
                                products.bank(key)[:].rearrange("p (c n) -> p c n", c=4).unsqueeze(2).to_broadcast([P, 4, 2, P]),
                                member[:, 0:2].unsqueeze(1).unsqueeze(3).to_broadcast([P, 4, 2, P]), ALU.mult), key)

                    elif kind == "qkv":
                        key = (kind, block, s, 0)
                        products.wait_full(dve, it, key)
                        qk = products.bank(key)[:].rearrange("p (h r) -> p h r", r=16)
                        ra, rb = (t[s].rearrange("p (h r) -> p h r", r=16) for t in (rope_a, rope_b))
                        nc.vector.tensor_tensor(ra, qk, rope[:, 0:16].unsqueeze(1).to_broadcast([P, 32, 16]), ALU.mult)
                        nc.vector.tensor_tensor(rb[:, :, 0:8], qk[:, :, 8:16], rope[:, 16:24].unsqueeze(1).to_broadcast([P, 32, 8]), ALU.mult)
                        ins = nc.vector.tensor_tensor(rb[:, :, 8:16], qk[:, :, 0:8], rope[:, 24:32].unsqueeze(1).to_broadcast([P, 32, 8]), ALU.mult)
                        products.empty(ins, key)
                        products.wait_emptied(dve, it, key)
                        nc.vector.tensor_tensor(roped[s], rope_a[s], rope_b[s], ALU.add).then_inc(s_roped, 1)
                        key = (kind, block, s, 1)
                        products.wait_full(dve, it, key)
                        products.empty(nc.vector.tensor_copy(vals[s][:, 0:D], products.bank(key)[:, 0:D]), key)

                    elif kind == "qkT":
                        key = (kind, block, s, 1)
                        products.wait_full(dve, it, key)
                        for c in range(DC):
                            ins = nc.vector.tensor_tensor(
                                keys[s][:, c * 1024:(c + 1) * 1024].rearrange("p (h n) -> p h n", h=8),
                                products.bank(key)[:, c * P:(c + 1) * P].unsqueeze(1).to_broadcast([P, 8, P]),
                                member[:, 2:10].unsqueeze(2).to_broadcast([P, 8, P]), ALU.mult)
                        products.empty(ins, key)

                    elif kind == "cqk":
                        key = (kind, block, s, 0)
                        products.wait_full(dve, it, key)
                        bank = products.bank(key)
                        nc.vector.tensor_scalar(queries[s][:, 0:P], bank[:, 0:P], HEAD[block] ** -0.5, None, ALU.mult)
                        nc.vector.tensor_copy(vals[s][:, 0:P], bank[:, 2 * P:3 * P])
                        products.empty(nc.vector.tensor_tensor(
                            keys[s][:].rearrange("p (h n) -> p h n", h=16), bank[:, P:2 * P].unsqueeze(1).to_broadcast([P, 16, P]),
                            member[:, 10:26].unsqueeze(2).to_broadcast([P, 16, P]), ALU.mult), key)

                    elif kind in ("wo", "ff2", "down"):
                        key = (kind, block, s, 0)
                        products.wait_full(dve, it, key)
                        bank = products.bank(key)
                        if block in ("one", "three"):
                            g = GATES.index(block + ("_ff" if kind == "ff2" else ""))
                            ins = nc.vector.scalar_tensor_tensor(out=x[s][:], in0=bank[:, 0:D], scalar=tanh_gates[:, g:g + 1], in1=x[s][:],
                                                                 op0=ALU.mult, op1=ALU.add)
                        elif block == "cross":
                            ins = nc.vector.tensor_tensor(x[s][:], bank[:, 0:D], x[s][:], ALU.add)
                        else:
                            link(nc.vector.scalar_tensor_tensor(out=x[s][:], in0=bank[:, 0:D], scalar=expert[s][:, 0:1], in1=x[s][:],
                                                                op0=ALU.mult, op1=ALU.add))
                            ins = nc.vector.scalar_tensor_tensor(out=x[s][:], in0=bank[:, D:2 * D], scalar=expert[s][:, 1:2], in1=x[s][:],
                                                                 op0=ALU.mult, op1=ALU.add)
                        products.empty(ins, key)
                        if (kind, block) != ("ff2", "three"):
                            products.wait_emptied(dve, it, key)
                            norm({("wo", "one"): "one_ff", ("ff2", "one"): "self", ("wo", "self"): "cross", ("wo", "cross"): "mlp",
                                  ("down", "mlp"): "three", ("wo", "three"): "three_ff"}[kind, block], s)

                    elif kind == "gu":
                        for i in range(2 * FC // 2):
                            key = (kind, block, s, i)
                            dve.wait_ge(s_silu, it * len(gu_no) + gu_no[s, i] + 1)
                            e, pair = i // (FC // 2), i % (FC // 2)
                            products.empty(nc.vector.tensor_tensor(hidden2[s][:, e, 2 * pair:2 * pair + 2, :],
                                                                   products.bank(key)[:, D:2 * D].rearrange("p (c n) -> p c n", c=2),
                                                                   silu[s][i % 2].rearrange("p (c n) -> p c n", c=2), ALU.mult), key)
                assert state["n"] == N_LINKS, (state["n"], N_LINKS)


def kernel(**inputs):
    import numpy as _np
    import concourse.bacc as _bacc
    from concourse import mybir as _mybir
    from concourse.bass_utils import run_bass_kernel_spmd as _run

    a = {name: _np.asarray(v) for name, v in inputs.items()}

    def by_chunk(m):
        return m.reshape(-1, P, m.shape[1]).transpose(1, 0, 2)

    L0, L1, L2, L3 = (f"L{i}_xattn_" for i in range(4))
    full = (FC - 1) * P
    arrays = {
        "x": a["x"],
        "xT": a["x"].reshape(BATCH, P, DC, P).transpose(0, 3, 2, 1),
        "ctxT": a["ctx_1024"].transpose(0, 2, 1),
        "keep": a["mask_BxS2_bk0"],
        "types": _np.stack([a["mask_BxS_ik0"], _np.pad(a["mask_BxS_ik0"][:, 1:], ((0, 0), (0, 1)))], axis=2),
        "positions": a["pos_1xS"],
        "mem": a[L0 + "W_mem"].T, "gate": by_chunk(a[L0 + "W_gate"].T),
        "gate_bias": a[L0 + "b_gate"][None], "fuse_gain": a[L0 + "norm_w"][None],
        "gates": _np.concatenate([a[L1 + "attn_gate"], a[L1 + "ff_gate"], a[L3 + "attn_gate"], a[L3 + "ff_gate"]])[None],
        "v_qkv": by_chunk(a[L2 + "v_qkv"]), "l_qkv": by_chunk(a[L2 + "l_qkv"]),
        "vl_dense": by_chunk(_np.concatenate([a[L2 + "v_dense"], a[L2 + "l_dense"]], axis=1)),
        "cq": by_chunk(a[L2 + "cq_w"]), "ckv": a[L2 + "ckv_w"], "cdense": a[L2 + "cdense_w"],
    }
    for name, pre in (("one", L1), ("three", L3)):
        arrays[name + "_q"] = by_chunk(a[pre + "Wq"])
        arrays[name + "_kv"] = a[pre + "Wkv"]
        arrays[name + "_o"] = by_chunk(a[pre + "Wo"])
        arrays[name + "_1"] = by_chunk(a[pre + "W1"])
        arrays[name + "_2"] = by_chunk(a[pre + "W2"])
    for e in "vl":
        arrays[e + "_gate"], arrays[e + "_up"] = by_chunk(a[L2 + e + "_gate"]), by_chunk(a[L2 + e + "_up"])
        arrays[e + "_down0"], arrays[e + "_down1"] = by_chunk(a[L2 + e + "_down"][:full]), a[L2 + e + "_down"][full:]
    gains = [(L1 + "ln_q_g", L1 + "ln_q_b"), (L1 + "ln_ff_g", L1 + "ln_ff_b"), (L2 + "ln_in_w",) * 2, (L2 + "ln_post_cross_w",) * 2,
             (L2 + "ln_post_attn_w",) * 2, (L3 + "ln_q_g", L3 + "ln_q_b"), (L3 + "ln_ff_g", L3 + "ln_ff_b")]
    arrays["features"] = _np.stack([_np.stack([a[n].reshape(DC, P) for n in pair]) for pair in gains]).transpose(3, 0, 1, 2)
    arrays["ident"] = _np.eye(P, dtype=_np.float32)
    rows = _np.arange(P)
    arrays["member"] = _np.concatenate([(rows[:, None] // w == _np.arange(P // w)) for w in (64, 16, 8)], axis=1).astype(_np.float32)
    arrays["row_number"] = rows[:, None].astype(_np.float32)
    arrays["causal"] = _np.where(rows[:, None] >= rows, 0.0, MASKED).astype(_np.float32)
    inverse = (1.0 / 10000.0 ** (_np.arange(0, 16, 2, dtype=_np.float32) / 16)).astype(_np.float32)
    angle = rows[:, None].astype(_np.float32) * inverse
    arrays["rope_rows"] = _np.concatenate([_np.cos(angle), _np.cos(angle), -_np.sin(angle), _np.sin(angle)], axis=1).astype(_np.float32)

    nc = _bacc.Bacc("TRN2", target_bir_lowering=False, num_devices=1)
    given, aps = {}, {}
    for name, v in arrays.items():
        given["in_" + name] = _np.ascontiguousarray(v)
        aps[name] = nc.dram_tensor("in_" + name, v.shape, _mybir.dt.from_np(v.dtype), kind="ExternalInput").ap()
    for e in "vl":
        aps[e + "_down"] = (aps[e + "_down0"], aps[e + "_down1"])
    out = nc.dram_tensor("out", a["x"].shape, _mybir.dt.float32, kind="ExternalOutput").ap()
    build(nc, aps, out)
    r = _run(nc, [given], core_ids=[0])
    return r.results[0]["out"]
```

```python
from contextlib import ExitStack

import concourse.bass as bass
from concourse import mybir

F32 = mybir.dt.float32
BF16 = mybir.dt.bfloat16
I32 = mybir.dt.int32
U8 = mybir.dt.uint8
ALU = mybir.AluOpType
ACT = mybir.ActivationFunctionType
AX = mybir.AxisListType

P = 128
BATCH = 8
SLOTS = 2
ITERATIONS = BATCH // SLOTS
D = 256
DC = D // P
INNER = 1024
IC = INNER // P
FF = 688
FC = -(-FF // P)
FREST = FF - (FC - 1) * P
HEADS = 16
GROUP = 4
UNITS = HEADS // GROUP
HEAD = {"one": 64, "self": 16, "cross": 8, "three": 64}
MASKED = -(2.0 ** 127)
EPS = {"fuse": 1e-6, "one": 1e-5, "one_ff": 1e-5, "self": 1e-6, "cross": 1e-6, "mlp": 1e-6,
       "three": 1e-5, "three_ff": 1e-5}
FEATURES = ["one", "one_ff", "self", "cross", "mlp", "three", "three_ff"]
GATES = ["one", "one_ff", "three", "three_ff"]
PRODUCT_BANKS = {(kind, block): n for kind, blocks, n in (
    ("mem", (None,), 1), ("mcT", (None,), 1), ("gate", (None,), 1), ("kv", ("one", "three"), 4),
    ("nT", ("one", "one_ff", "self", "cross", "mlp", "three", "three_ff"), 1), ("q", ("one", "three"), 2),
    ("qkv", ("self",), 2), ("qkT", ("self",), 2), ("cqk", ("cross",), 1), ("oT", ("one", "three"), 2),
    ("oT", ("self", "cross"), 1), ("wo", ("one", "self", "cross", "three"), 1), ("ff1", ("one", "three"), 2),
    ("ff2", ("one", "three"), 1), ("gu", ("mlp",), FC), ("down", ("mlp",), 1)) for block in blocks}
STATISTICS = {("gate", None): "fuse", ("xn", "fuse"): "one", ("wo", "one"): "one_ff", ("ff2", "one"): "self",
              ("wo", "self"): "cross", ("wo", "cross"): "mlp", ("down", "mlp"): "three", ("wo", "three"): "three_ff"}
CENTRED = ("one", "one_ff", "three", "three_ff")
LINKS = {("mem", None): 2, ("gate", None): 2, ("xn", "fuse"): 1, ("xn", "self"): 2, ("wo", "self"): 1, ("down", "mlp"): 1}
VALUES_LINKS = 1
STATISTICS_LINKS = {True: 1, False: 2}


ORDER = """
mem:A0 mem:B0 scores.fuse:A0 kv.one:A2 scores.fuse:B0 kv.one:A1 turn.fuse:A0 values.fuse:A0 turn.fuse:B0 mcT:A0
values.fuse:B0 kv.one:A0 gate:A0 mcT:B0 xn.fuse:A0 kv.one:B3 xn.one:A0 gate:B0 kv.one:B1 kv.one:A3 nT.one:A0
kv.one:B2 xn.fuse:B0 q.one:A0 kv.one:B0 scores.one:A0 q.one:A1 scores.one:A1 turn.one:A0 xn.one:B0 scores.one:A2
values.one:A0 nT.one:B0 turn.one:A1 scores.one:A3 values.one:A1 turn.one:A2 q.one:B0 turn.one:A3 values.one:A2
oT.one:A0 values.one:A3 scores.one:B0 oT.one:A1 scores.one:B1 wo.one:A0 q.one:B1 xn.one_ff:A0 turn.one:B0
turn.one:B1 scores.one:B2 nT.one_ff:A0 scores.one:B3 values.one:B0 values.one:B1 turn.one:B2 ff1.one:A0
turn.one:B3 values.one:B2 oT.one:B0 values.one:B3 ff1.one:A1 oT.one:B1 wo.one:B0 xn.one_ff:B0 ff2.one:A0
nT.one_ff:B0 xn.self:A0 ff1.one:B0 ff1.one:B1 nT.self:A0 ff2.one:B0 xn.self:B0 qkv.self:A0 qkv.self:A1
nT.self:B0 qkT.self:A0 qkT.self:A1 qkv.self:B0 scores.self:A0 qkv.self:B1 scores.self:A1 qkT.self:B0 qkT.self:B1
turn.self:A0 scores.self:A2 turn.self:A1 values.self:A0 scores.self:A3 values.self:A1 turn.self:A2
scores.self:B0 values.self:A2 turn.self:A3 scores.self:B1 values.self:A3 turn.self:B0 oT.self:A0 scores.self:B2
turn.self:B1 wo.self:A0 scores.self:B3 xn.cross:A0 values.self:B0 values.self:B1 turn.self:B2 nT.cross:A0
turn.self:B3 values.self:B2 values.self:B3 oT.self:B0 cqk.cross:A0 wo.self:B0 scores.cross:A0 scores.cross:A1
xn.cross:B0 nT.cross:B0 turn.cross:A0 scores.cross:A2 turn.cross:A1 scores.cross:A3 cqk.cross:B0 values.cross:A0
values.cross:A1 turn.cross:A2 turn.cross:A3 scores.cross:B0 scores.cross:B1 values.cross:A2 values.cross:A3
kv.three:A3 turn.cross:B0 oT.cross:A0 scores.cross:B2 turn.cross:B1 scores.cross:B3 wo.cross:A0 values.cross:B0
turn.cross:B2 values.cross:B1 kv.three:A1 turn.cross:B3 xn.mlp:A0 values.cross:B2 values.cross:B3 nT.mlp:A0
oT.cross:B0 wo.cross:B0 gu.mlp:A0 xn.mlp:B0 kv.three:B3 nT.mlp:B0 gu.mlp:A1 gu.mlp:A2 gu.mlp:A3 gu.mlp:B0
gu.mlp:A4 gu.mlp:A5 gu.mlp:B1 down.mlp:A0 gu.mlp:B2 gu.mlp:B3 gu.mlp:B4 xn.three:A0 kv.three:B1 nT.three:A0
kv.three:A2 q.three:A0 kv.three:A0 gu.mlp:B5 scores.three:A0 scores.three:A1 down.mlp:B0 xn.three:B0 q.three:A1
kv.three:B2 turn.three:A0 turn.three:A1 nT.three:B0 scores.three:A2 kv.three:B0 q.three:B0 scores.three:A3
values.three:A0 turn.three:A2 values.three:A1 scores.three:B0 turn.three:A3 oT.three:A0 values.three:A2
values.three:A3 turn.three:B0 q.three:B1 oT.three:A1 scores.three:B1 wo.three:A0 scores.three:B2 turn.three:B1
xn.three_ff:A0 scores.three:B3 values.three:B0 values.three:B1 nT.three_ff:A0 turn.three:B2 oT.three:B0
turn.three:B3 values.three:B2 values.three:B3 ff1.three:A0 oT.three:B1 wo.three:B0 xn.three_ff:B0 ff1.three:A1
ff2.three:A0 nT.three_ff:B0 ff1.three:B0 ff1.three:B1 ff2.three:B0
"""


def steps():
    out = []
    for word in ORDER.split():
        what, where = word.split(":")
        kind, _, block = what.partition(".")
        out.append((kind, block or None, "AB".index(where[0]), int(where[1:])))
    return out


class Pool:

    def __init__(self, banks, full, emptied):
        self.banks, self.full, self.emptied = banks, full, emptied
        self.uses = [0] * len(banks)
        self.of = {}
        self.n = 0
        self.waited = {}

    def plan(self, key):
        b = self.n % len(self.banks)
        self.of[key] = (b, self.uses[b])
        self.uses[b] += 1
        self.n += 1

    def bank(self, key):
        return self.banks[self.of[key][0]]

    def wait_before(self, eng, it, key):
        b, k = self.of[key]
        self.waited[b] = k
        eng.wait_ge(self.emptied[b], it * self.uses[b] + k + 1)

    def wait_full(self, eng, it, key):
        b, k = self.of[key]
        eng.wait_ge(self.full[b], it * self.uses[b] + k + 2)

    def wait_full_before(self, eng, it, key):
        b, k = self.of[key]
        eng.wait_ge(self.full[b], it * self.uses[b] + k + 1)

    def wait_emptied(self, eng, it, key):
        b, k = self.of[key]
        eng.wait_ge(self.emptied[b], it * self.uses[b] + k + 2)

    def filled(self, ins, key):
        ins.then_inc(self.full[self.of[key][0]], 1)

    def empty(self, ins, key):
        ins.then_inc(self.emptied[self.of[key][0]], 1)


def build(nc, a, out):
    STEPS = steps()
    with ExitStack() as ctx:
        def sb(name, shape, dt=F32):
            return ctx.enter_context(nc.sbuf_tensor(name, shape, dt))

        def sem(name):
            return ctx.enter_context(nc.semaphore(name))

        w = {name: sb("w_" + name, shape) for name, shape in {
            "mem": [P, D], "gate": [P, 2 * DC, D],
            "one_q": [P, DC, INNER], "one_kv": [P, 2 * INNER], "one_o": [P, IC, D],
            "one_1": [P, DC, INNER], "one_2": [P, IC, D],
            "v_qkv": [P, DC, 3 * D], "l_qkv": [P, DC, 3 * D], "vl_dense": [P, DC, 2 * D],
            "cq": [P, DC, P], "ckv": [P, 2 * P], "cdense": [P, D],
            "v_gate": [P, DC, FC * P], "v_up": [P, DC, FC * P], "l_gate": [P, DC, FC * P], "l_up": [P, DC, FC * P],
            "v_down": [P, FC, D], "l_down": [P, FC, D],
            "three_q": [P, DC, INNER], "three_kv": [P, 2 * INNER], "three_o": [P, IC, D],
            "three_1": [P, DC, INNER], "three_2": [P, IC, D]}.items()}
        features = sb("features", [P, len(FEATURES), 2, DC])
        gates = sb("gates", [P, len(GATES)])
        tanh_gates = sb("tanh_gates", [P, len(GATES)])
        fuse_gain = sb("fuse_gain", [P, D])
        gate_bias = sb("gate_bias", [1, D])
        ones_row = sb("ones_row", [1, P])
        ones_row_bf = sb("ones_row_bf", [1, P], BF16)
        minus_half = sb("minus_half", [P, 1])
        ident = sb("ident", [P, P])
        ident_bf = sb("ident_bf", [P, P], BF16)
        member = sb("member", [P, 2 + 8 + 16])
        row_number = sb("row_number", [P, 1])
        causal = sb("causal", [P, P], BF16)
        rope = sb("rope", [P, 32])

        slots = range(SLOTS)
        x_in = [sb(f"x_in{s}", [P, D]) for s in slots]
        x_inT = [sb(f"x_inT{s}", [P, DC, P]) for s in slots]
        ctxT = [sb(f"ctxT{s}", [P, P]) for s in slots]
        keep_in = [sb(f"keep_in{s}", [1, P], U8) for s in slots]
        keep = [sb(f"keep{s}", [1, P], BF16) for s in slots]
        types = [sb(f"types{s}", [P, 2], I32) for s in slots]
        expert = [sb(f"expert{s}", [P, 4]) for s in slots]
        x = [sb(f"x{s}", [P, D]) for s in slots]
        xnT = [sb(f"xnT{s}", [P, DC, 2, P]) for s in slots]
        keys = [sb(f"keys{s}", [P, 2048]) for s in slots]
        queries = [sb(f"queries{s}", [P, INNER]) for s in slots]
        vals = [sb(f"vals{s}", [P, INNER]) for s in slots]
        heads = [sb(f"heads{s}", [P, INNER]) for s in slots]
        xn = [heads[s][:, 0:2 * D].rearrange("p (v d) -> p v d", v=2) for s in slots]
        context = [heads[s][:, 2 * D:3 * D] for s in slots]
        contextT = [queries[s][:, 0:DC * P].rearrange("p (c n) -> p c n", c=DC) for s in slots]
        memT = [heads[s][:, 0:DC * P].rearrange("p (c n) -> p c n", c=DC) for s in slots]
        mem = [heads[s][:, D:2 * D] for s in slots]
        gate_tanh = [queries[s][:, D:2 * D] for s in slots]
        gated = [queries[s][:, 2 * D:3 * D] for s in slots]
        hidden = [keys[s][:, 0:INNER].rearrange("p (c n) -> p c n", c=IC) for s in slots]
        hidden2 = [keys[s][:, 0:2 * FC * P].rearrange("p (e c n) -> p e c n", e=2, c=FC) for s in slots]
        roped = [keys[s][:, 0:2 * D] for s in slots]
        rope_a = [heads[s][:, 0:2 * D] for s in slots]
        rope_b = [heads[s][:, 2 * D:4 * D] for s in slots]
        silu = [[heads[s][:, D * b:D * b + D] for b in range(2)] for s in slots]
        probs = [sb(f"probs{i}", [P, GROUP, P]) for i in range(2)]
        probsT = [sb(f"probsT{i}", [P, GROUP, P]) for i in range(2)]

        causal_f = probs[0][:, 0, :]
        positions = probs[0][:, 1, :].bitcast(I32)
        tmp_pos = probs[0][:, 2:4, :]
        rope_rows = probs[1][:, 0, 0:32]

        def psum_pool(name, n):
            return Pool([ctx.enter_context(nc.psum_tensor(f"{name}{i}", [P, 512], F32)) for i in range(n)],
                        [sem(f"{name}_full{i}") for i in range(n)], [sem(f"{name}_emptied{i}") for i in range(n)])

        products, scores, turned, values = (psum_pool(n, 2) for n in ("products", "scores", "turned", "values"))

        unit_no, norm_no, xn_no, roped_no, gu_no = {}, {}, {}, {}, {}
        for kind, block, s, i in STEPS:
            if kind == "scores":
                unit_no[block, s, i] = len(unit_no)
                scores.plan((block, s, i))
            elif kind == "turn":
                turned.plan((block, s, i))
            elif kind == "values":
                values.plan((block, s, i))
            elif kind == "xn":
                if block != "fuse":
                    xn_no[block, s] = len(xn_no)
            else:
                products.plan((kind, block, s, i))
                if (kind, i) == ("qkv", 0):
                    roped_no[s] = len(roped_no)
                if kind == "gu":
                    gu_no[s, i] = len(gu_no)
            if (kind, block) in STATISTICS:
                norm_no[STATISTICS[kind, block], s] = len(norm_no)
        N_UNITS, N_NORMS = len(unit_no), len(norm_no)
        N_LINKS = 0
        for kind, block, s, i in STEPS:
            N_LINKS += LINKS.get((kind, block), 0) + VALUES_LINKS * (kind == "values")
            if (kind, block) in STATISTICS:
                N_LINKS += STATISTICS_LINKS[STATISTICS[kind, block] in CENTRED]

        moments = sb("moments", [P, N_NORMS, 6])
        mean_var = sb("mean_var", [P, N_NORMS, 2])
        square = sb("square", [P, N_NORMS])
        var_eps = sb("var_eps", [P, N_NORMS])
        rstd = sb("rstd", [P, N_NORMS])
        rstd_expert = sb("rstd_expert", [P, SLOTS, 2])
        minus_max = sb("minus_max", [P, N_UNITS, GROUP])
        total = sb("total", [P, N_UNITS, GROUP])
        inv_total = sb("inv_total", [P, N_UNITS, GROUP])

        s_weights = {g: sem("weights_loaded_" + g) for g in ("fuse", "one_kv", "one", "one_ff", "two_a", "two_mlp", "three")}
        n_weights = dict.fromkeys(s_weights, 0)
        s_pads = sem("weight_pads_zeroed")
        s_consts = sem("constants_loaded")
        s_set = sem("constants_set")
        s_onehot = sem("positions_one_hot")
        s_rope_full = sem("rope_rows_gathered")
        s_rope = sem("rope_ready")
        s_tanh_gates = sem("tanh_gates_ready")
        s_x = [sem(f"x_loaded{s}") for s in slots]
        s_side = [sem(f"side_inputs_loaded{s}") for s in slots]
        s_x_used = [sem(f"x_input_used{s}") for s in slots]
        s_side_used = [sem(f"side_inputs_used{s}") for s in slots]
        s_keep = sem("key_masks_ready")
        s_link = sem("vector_done")
        s_var = sem("variance_ready")
        s_rstd = sem("rstd_ready")
        s_xn = sem("normalised_ready")
        s_max = sem("minus_max_ready")
        s_roped = sem("roped_ready")
        s_silu = sem("silu_ready")
        s_stored = [sem(f"result_stored{s}") for s in slots]
        s_x_free = [sem(f"x_free{s}") for s in slots]

        block_ = ctx.enter_context(nc.Block())

        WEIGHTS = [("fuse", "mem"), ("fuse", "gate"), ("one_kv", "one_kv"), ("one", "one_q"), ("one", "one_o"),
                   ("one_ff", "one_1"), ("one_ff", "one_2"), ("two_a", "v_qkv"), ("two_a", "l_qkv"),
                   ("two_a", "vl_dense"), ("two_a", "cq"), ("two_a", "ckv"), ("two_a", "cdense"),
                   ("two_mlp", "v_gate"), ("two_mlp", "v_up"), ("two_mlp", "l_gate"), ("two_mlp", "l_up"),
                   ("two_mlp", "v_down"), ("two_mlp", "l_down"), ("three", "three_kv"), ("three", "three_q"),
                   ("three", "three_o"), ("three", "three_1"), ("three", "three_2")]
        for group, name in WEIGHTS:
            n_weights[group] += 32 if name.endswith("_down") else 16
        CONSTS = [(features[:], a["features"]), (gates[:], a["gates"].partition_broadcast(P)),
                  (fuse_gain[:], a["fuse_gain"].partition_broadcast(P)), (gate_bias[:], a["gate_bias"]),
                  (ident[:], a["ident"]), (causal_f, a["causal"]), (member[:], a["member"]),
                  (row_number[:], a["row_number"]), (rope_rows, a["rope_rows"]),
                  (positions, a["positions"].partition_broadcast(P))]

        def load_weight(sp, group, name):
            if name.endswith("_down"):
                sp.dma_start(w[name][:, 0:FC - 1, :], a[name][0]).then_inc(s_weights[group], 16)
                sp.dma_start(w[name][0:FREST, FC - 1, :], a[name][1]).then_inc(s_weights[group], 16)
            elif name.endswith("_gate") or name.endswith("_up"):
                sp.dma_start(w[name][:, :, 0:FF], a[name]).then_inc(s_weights[group], 16)
            else:
                sp.dma_start(w[name][:], a[name]).then_inc(s_weights[group], 16)

        @block_.sync
        def _(sp):
            for group, name in WEIGHTS[:2]:
                load_weight(sp, group, name)

            def load_x(it, s):
                sp.wait_ge(s_x_used[s], it + 1)
                b = it * SLOTS + s
                sp.dma_start(x_in[s][:], a["x"][bass.ds(b, 1), :, :].rearrange("o p n -> p (o n)")).then_inc(s_x[s], 16)
                sp.dma_start(x_inT[s][:], a["xT"][bass.ds(b, 1), :, :, :].rearrange("o p c n -> p (o c) n")).then_inc(s_x[s], 16)

            def load_side(it, s):
                sp.wait_ge(s_side_used[s], it + 1)
                b = it * SLOTS + s
                sp.dma_start(ctxT[s][:], a["ctxT"][bass.ds(b, 1), :, :].rearrange("o p n -> p (o n)")).then_inc(s_side[s], 16)
                sp.dma_start(keep_in[s][:], a["keep"][bass.ds(b, 1), :]).then_inc(s_side[s], 16)
                sp.dma_start(types[s][:], a["types"][bass.ds(b, 1), :, :].rearrange("o p n -> p (o n)")).then_inc(s_side[s], 16)

            with sp.Fori(0, ITERATIONS) as it:
                for s in slots:
                    load_x(it, s)
                for s in slots:
                    load_side(it, s)

        @block_.gpsimd
        def _(pool):
            for p in (products, scores, turned, values):
                for q in (*p.full, *p.emptied):
                    pool.sem_inc(q, 1)
            for q in (*s_x_used, *s_side_used, *s_x_free):
                pool.sem_inc(q, 1)
            nc.gpsimd.memset(minus_half[:], -0.5).then_inc(s_set, 1)
            pool.wait_ge(s_set, 1)
            with pool.Fori(0, ITERATIONS) as it:
                for kind, block, s, _ in STEPS:
                    if (kind, block) in STATISTICS:
                        n = norm_no[STATISTICS[kind, block], s]
                        pool.wait_ge(s_var, it * N_NORMS + n + 1)
                        nc.gpsimd.tensor_tensor(rstd[:, n:n + 1], var_eps[:, n:n + 1], minus_half[:],
                                                ALU.pow).then_inc(s_rstd, 1)
                    if kind == "ff2" and block == "three":
                        pool.wait_ge(s_set, 1)
                        products.wait_emptied(pool, it, (kind, block, s, 0))
                        b = it * SLOTS + s
                        pool.dma_start(out[bass.ds(b, 1), :, :].rearrange("o p n -> p (o n)"), x[s][:]).then_inc(s_stored[s], 16)
                        pool.wait_ge(s_stored[s], (it + 1) * 16)
                        pool.sem_inc(s_x_free[s], 1)

        @block_.tensor
        def _(pe):
            mm = nc.tensor.matmul

            def have(group):
                pe.wait_ge(s_weights[group], n_weights[group])

            pe.wait_ge(s_onehot, 1)
            mm(values.banks[0][:, 0:32], tmp_pos[:, 1, :], rope_rows, start=True, stop=True).then_inc(s_rope_full, 1)
            pe.wait_ge(s_rope, 1)
            pe.wait_ge(s_pads, 6)

            with pe.Fori(0, ITERATIONS) as it:
                def fill(kind, block, s, i):
                    key = (kind, block, s, i)
                    products.wait_before(pe, it, key)
                    return key, products.bank(key)

                def copied(*sources):
                    for source in sources:
                        b, k = products.of[source]
                        if products.waited.get(b, -1) <= k:
                            products.wait_emptied(pe, it, source)
                            products.waited[b] = k + 1

                for kind, block, s, i in STEPS:
                    if kind == "mem":
                        pe.wait_ge(s_side[s], (it + 1) * 48)
                        have("fuse")
                        key, bank = fill(kind, block, s, 0)
                        for c in range(DC):
                            mm(bank[:, c * P:(c + 1) * P], w["mem"][:, c * P:(c + 1) * P], ctxT[s][:], start=True, stop=True)
                        products.filled(mm(bank[:, D:2 * D], ctxT[s][:], w["mem"][:], start=True, stop=True), key)

                    elif kind == "scores":
                        key = (block, s, i)
                        scores.wait_before(pe, it, key)
                        bank = scores.bank(key)
                        u = i
                        if block == "fuse":
                            pe.wait_ge(s_x[s], (it + 1) * 32)
                            copied(("mem", None, s, 0))
                            for c in range(DC):
                                last = mm(bank[:, 0:P], x_inT[s][:, c, :], memT[s][:, c, :], start=(c == 0), stop=(c == DC - 1))
                        elif block == "self":
                            if u == 0:
                                copied(("qkT", block, s, 0), ("qkT", block, s, 1))
                            mm(bank[:], ident_bf[:], causal[:].unsqueeze(1).to_broadcast([P, GROUP, P]), start=True, stop=False)
                            t = u // 2
                            last = mm(bank[:], queries[s][:, t * P:(t + 1) * P],
                                      keys[s][:, u * 512:(u + 1) * 512], start=False, stop=True)
                        elif block == "cross":
                            if u == 0:
                                copied(("cqk", block, s, 0))
                            last = mm(bank[:], queries[s][:, 0:P], keys[s][:, u * 512:(u + 1) * 512], start=True, stop=True)
                        else:
                            if u == 0:
                                copied(("kv", block, s, 3), ("kv", block, s, 2), ("kv", block, s, 1), ("kv", block, s, 0))
                                pe.wait_ge(s_keep, it * SLOTS + s + 1)
                            if u % 2 == 0:
                                copied(("q", block, s, u // 2))
                            mm(bank[:], ones_row_bf[:], keep[s][:].unsqueeze(1).to_broadcast([1, GROUP, P]), start=True, stop=False)
                            for j in range(2):
                                t = 2 * u + j
                                last = mm(bank[:, j * 256:(j + 1) * 256], queries[s][:, t * P:(t + 1) * P],
                                          keys[s][:, t * 256:(t + 1) * 256], start=False, stop=(j == 1))
                        scores.filled(last, key)

                    elif kind == "turn":
                        key = (block, s, i)
                        turned.wait_before(pe, it, key)
                        scores.wait_emptied(pe, it, key)
                        b = turned.of[key][0]
                        for j in range(1 if block == "fuse" else GROUP):
                            last = nc.tensor.transpose(turned.bank(key)[:, j * P:(j + 1) * P], probs[b][:, j, :], ident[:])
                        turned.filled(last, key)

                    elif kind == "values":
                        key = (block, s, i)
                        values.wait_before(pe, it, key)
                        turned.wait_emptied(pe, it, key)
                        b = turned.of[key][0]
                        bank = values.bank(key)
                        if block == "fuse":
                            last = mm(bank[:, 0:D], probsT[b][:, 0, :], mem[s], start=True, stop=True)
                        else:
                            h = HEAD[block]
                            for j in range(GROUP):
                                c = (i * GROUP + j) * h
                                last = mm(bank[:, j * h:(j + 1) * h], probsT[b][:, j, :], vals[s][:, c:c + h], start=True, stop=True)
                                if block == "three" and i == UNITS - 1 and j == 0:
                                    last.then_inc(s_side_used[s], 1)
                        values.filled(last, key)

                    elif kind == "mcT":
                        key, bank = fill(kind, block, s, 0)
                        values.wait_emptied(pe, it, ("fuse", s, 0))
                        for c in range(DC):
                            last = nc.tensor.transpose(bank[:, c * P:(c + 1) * P], context[s][:, c * P:(c + 1) * P], ident[:])
                        products.filled(last, key)

                    elif kind == "gate":
                        key, bank = fill(kind, block, s, 0)
                        copied(("mcT", block, s, 0))
                        mm(bank[:, 0:D], ones_row[:], gate_bias[:], start=True, stop=False)
                        for c in range(2 * DC):
                            lhs = x_inT[s][:, c, :] if c < DC else contextT[s][:, c - DC, :]
                            last = mm(bank[:, 0:D], lhs, w["gate"][:, c, :], start=False, stop=(c == 2 * DC - 1))
                        products.filled(last, key)

                    elif kind == "kv":
                        wkv = w[block + "_kv"]
                        have("one_kv" if block == "one" else "three")
                        key, bank = fill(kind, block, s, i)
                        if i % 2 == 0:
                            for j in range(4):
                                t = 2 * i + j
                                last = mm(bank[:, j * P:(j + 1) * P], wkv[:, t * P:(t + 1) * P], ctxT[s][:], start=True, stop=True)
                        else:
                            c = INNER + (i // 2) * 512
                            last = mm(bank[:], ctxT[s][:], wkv[:, c:c + 512], start=True, stop=True)
                        products.filled(last, key)

                    elif kind == "nT":
                        key, bank = fill(kind, block, s, 0)
                        pe.wait_ge(s_xn, it * len(xn_no) + xn_no[block, s] + 1)
                        nv = 2 if block == "self" else 1
                        for c in range(DC):
                            for v in range(nv):
                                last = nc.tensor.transpose(bank[:, (c * nv + v) * P:(c * nv + v + 1) * P],
                                                           xn[s][:, v, c * P:(c + 1) * P], ident[:])
                                if block == "one" and c == 0:
                                    last.then_inc(s_x_used[s], 1)
                        products.filled(last, key)

                    elif kind in ("q", "ff1"):
                        name = block + ("_q" if kind == "q" else "_1")
                        have({"one_q": "one", "one_1": "one_ff"}.get(name, "three"))
                        key, bank = fill(kind, block, s, i)
                        copied(("nT", block + ("_ff" if kind == "ff1" else ""), s, 0))
                        for j in range(4):
                            t = 4 * i + j
                            for c in range(DC):
                                last = mm(bank[:, j * P:(j + 1) * P], w[name][:, c, t * P:(t + 1) * P], xnT[s][:, c, 0, :],
                                          start=(c == 0), stop=(c == DC - 1))
                        products.filled(last, key)

                    elif kind == "qkv":
                        have("two_a")
                        key, bank = fill(kind, block, s, i)
                        copied(("nT", block, s, 0))
                        c0, n = ((0, 2 * D), (2 * D, D))[i]
                        k = 0
                        for v, name in enumerate(("v_qkv", "l_qkv")):
                            for c in range(DC):
                                last = mm(bank[:, 0:n], xnT[s][:, c, v, :], w[name][:, c, c0:c0 + n], start=(k == 0), stop=(k == 3))
                                k += 1
                        products.filled(last, key)

                    elif kind == "qkT":
                        key, bank = fill(kind, block, s, i)
                        pe.wait_ge(s_roped, it * SLOTS + roped_no[s] + 1)
                        for c in range(DC):
                            last = nc.tensor.transpose(bank[:, c * P:(c + 1) * P], roped[s][:, (i * DC + c) * P:(i * DC + c + 1) * P], ident[:])
                        products.filled(last, key)

                    elif kind == "cqk":
                        key, bank = fill(kind, block, s, 0)
                        mm(bank[:, P:2 * P], w["ckv"][:, 0:P], ctxT[s][:], start=True, stop=True)
                        mm(bank[:, 2 * P:3 * P], ctxT[s][:], w["ckv"][:, P:2 * P], start=True, stop=True)
                        copied(("nT", block, s, 0))
                        for c in range(DC):
                            last = mm(bank[:, 0:P], w["cq"][:, c, :], xnT[s][:, c, 0, :], start=(c == 0), stop=(c == DC - 1))
                        products.filled(last, key)

                    elif kind == "oT":
                        n = HEAD[block] * HEADS // P
                        values.wait_emptied(pe, it, (block, s, UNITS - 1 if n <= 4 else (i + 1) * UNITS // 2 - 1))
                        key, bank = fill(kind, block, s, i)
                        for j in range(min(4, n)):
                            t = 4 * i + j
                            last = nc.tensor.transpose(bank[:, j * P:(j + 1) * P], heads[s][:, t * P:(t + 1) * P], ident[:])
                        products.filled(last, key)

                    elif kind in ("wo", "ff2"):
                        key, bank = fill(kind, block, s, 0)
                        if kind == "wo":
                            n = HEAD[block] * HEADS // P
                            have({"one": "one", "three": "three"}.get(block, "two_a"))
                            source = ("oT", block, s)
                            weight = {"self": w["vl_dense"], "cross": w["cdense"][:].unsqueeze(1)}.get(block)
                            weight = w[block + "_o"] if weight is None else weight
                            lhs = [queries[s][:, t * P:(t + 1) * P] for t in range(n)]
                        else:
                            n = IC
                            have({"one": "one_ff"}.get(block, "three"))
                            source = ("ff1", block, s)
                            weight = w[block + "_2"]
                            lhs = [hidden[s][:, t, :] for t in range(n)]
                        width = 2 * D if block == "self" else D
                        for t in range(n):
                            if t % 4 == 0:
                                copied((*source, t // 4))
                            last = mm(bank[:, 0:width], lhs[t], weight[:, t, :], start=(t == 0), stop=(t == n - 1))
                        products.filled(last, key)

                    elif kind == "gu":
                        have("two_mlp")
                        key, bank = fill(kind, block, s, i)
                        copied(("nT", block, s, 0))
                        e, pair = "vl"[i // (FC // 2)], i % (FC // 2)
                        for g, name in enumerate(("_gate", "_up")):
                            for j in range(2):
                                t = 2 * pair + j
                                for c in range(DC):
                                    last = mm(bank[:, (2 * g + j) * P:(2 * g + j + 1) * P], w[e + name][:, c, t * P:(t + 1) * P],
                                              xnT[s][:, c, 0, :], start=(c == 0), stop=(c == DC - 1))
                        products.filled(last, key)

                    elif kind == "down":
                        key, bank = fill(kind, block, s, 0)
                        copied(("gu", block, s, FC - 1))
                        for e, name in enumerate(("v_down", "l_down")):
                            for t in range(FC):
                                last = mm(bank[:, e * D:(e + 1) * D], hidden2[s][:, e, t, :], w[name][:, t, :], start=(t == 0), stop=(t == FC - 1))
                        products.filled(last, key)

        @block_.scalar
        def _(act):
            for group, name in WEIGHTS[2:5]:
                load_weight(act, group, name)
            for dst, src in CONSTS:
                act.dma_start(dst, src).then_inc(s_consts, 16)
            act.wait_ge(s_pads, 6)
            for group, name in WEIGHTS[5:]:
                load_weight(act, group, name)
            act.wait_ge(s_consts, 16 * len(CONSTS))
            nc.scalar.activation(tanh_gates[:], gates[:], ACT.Tanh).then_inc(s_tanh_gates, 1)

            with act.Fori(0, ITERATIONS) as it:
                for kind, block, s, i in STEPS:
                    if kind == "mem":
                        key = (kind, block, s, 0)
                        products.wait_full(act, it, key)
                        bank = products.bank(key)
                        nc.scalar.activation(memT[s], bank[:, 0:D].rearrange("p (c n) -> p c n", c=DC), ACT.Copy, scale=D ** -0.5)
                        products.empty(nc.scalar.activation(mem[s], bank[:, D:2 * D], ACT.Copy), key)

                    elif kind == "scores":
                        key = (block, s, i)
                        n = unit_no[key]
                        act.wait_ge(s_max, it * N_UNITS + n + 1)
                        turned.wait_full_before(act, it, key)
                        b = turned.of[key][0]
                        for j in range(1 if block == "fuse" else GROUP):
                            last = nc.scalar.activation(probs[b][:, j, :], scores.bank(key)[:, j * P:(j + 1) * P], ACT.Exp,
                                                        bias=minus_max[:, n, j:j + 1], accum_out=total[:, n, j:j + 1])
                        scores.empty(last, key)

                    elif kind == "mcT":
                        key = (kind, block, s, 0)
                        products.wait_full(act, it, key)
                        products.empty(nc.scalar.activation(contextT[s], products.bank(key)[:, 0:D].rearrange("p (c n) -> p c n", c=DC),
                                                            ACT.Copy), key)

                    elif kind == "gate":
                        key = (kind, block, s, 0)
                        products.wait_full(act, it, key)
                        products.empty(nc.scalar.activation(gate_tanh[s], products.bank(key)[:, 0:D], ACT.Tanh, scale=0.5), key)

                    elif kind == "kv" and i % 2 == 1:
                        key = (kind, block, s, i)
                        products.wait_full(act, it, key)
                        products.empty(nc.scalar.activation(vals[s][:, (i // 2) * 512:(i // 2 + 1) * 512], products.bank(key)[:], ACT.Copy), key)

                    elif kind == "nT":
                        key = (kind, block, s, 0)
                        products.wait_full(act, it, key)
                        nv = 2 if block == "self" else 1
                        f = FEATURES.index(block)
                        for c in range(DC):
                            src = products.bank(key)[:, c * nv * P:(c + 1) * nv * P].rearrange("p (v n) -> p v n", v=nv)
                            if block in ("self", "cross", "mlp"):
                                last = nc.scalar.activation(xnT[s][:, c, 0:nv, :], src, ACT.Copy, scale=features[:, f, 0, c:c + 1])
                            else:
                                last = nc.scalar.activation(xnT[s][:, c, 0:nv, :], src, ACT.Identity, scale=features[:, f, 0, c:c + 1],
                                                            bias=features[:, f, 1, c:c + 1])
                        products.empty(last, key)

                    elif kind == "q":
                        key = (kind, block, s, i)
                        products.wait_full(act, it, key)
                        products.empty(nc.scalar.activation(queries[s][:, i * 512:(i + 1) * 512], products.bank(key)[:], ACT.Copy,
                                                            scale=HEAD[block] ** -0.5), key)

                    elif kind == "qkT" and i == 0:
                        key = (kind, block, s, 0)
                        products.wait_full(act, it, key)
                        products.empty(nc.scalar.activation(queries[s][:, 0:D], products.bank(key)[:, 0:D], ACT.Copy,
                                                            scale=HEAD[block] ** -0.5), key)

                    elif kind == "oT":
                        n = HEAD[block] * HEADS // P
                        key = (kind, block, s, i)
                        m = min(n, 4) * P
                        products.wait_full(act, it, key)
                        products.empty(nc.scalar.activation(queries[s][:, i * 512:i * 512 + m], products.bank(key)[:, 0:m], ACT.Copy), key)

                    elif kind == "ff1":
                        key = (kind, block, s, i)
                        products.wait_full(act, it, key)
                        products.empty(nc.scalar.activation(hidden[s][:, 4 * i:4 * i + 4, :], products.bank(key)[:].rearrange("p (c n) -> p c n", c=4),
                                                            ACT.Gelu), key)

                    elif kind == "gu":
                        key = (kind, block, s, i)
                        products.wait_full(act, it, key)
                        nc.scalar.activation(silu[s][i % 2], products.bank(key)[:, 0:D], ACT.Silu).then_inc(s_silu, 1)

        @block_.vector
        def _(dve):
            state = {"n": 0, "it": 0}

            def link(ins):
                state["n"] += 1
                ins.then_inc(s_link, 1)
                dve.wait_ge(s_link, state["it"] * N_LINKS + SETUP_LINKS + state["n"])

            SETUP_LINKS = 4
            for e in "vl":
                nc.vector.memset(w[e + "_gate"][:, :, FF:FC * P], 0.0).then_inc(s_pads, 1)
                nc.vector.memset(w[e + "_up"][:, :, FF:FC * P], 0.0).then_inc(s_pads, 1)
                nc.vector.memset(w[e + "_down"][:, FC - 1, :], 0.0).then_inc(s_pads, 1)
            nc.vector.memset(ones_row[:], 1.0)
            nc.vector.memset(ones_row_bf[:], 1.0)
            dve.wait_ge(s_consts, 16 * len(CONSTS))
            nc.vector.tensor_copy(ident_bf[:], ident[:])
            nc.vector.tensor_copy(causal[:], causal_f)

            def setup_link(ins, n):
                ins.then_inc(s_link, 1)
                dve.wait_ge(s_link, n)

            setup_link(nc.vector.tensor_scalar(tmp_pos[:, 1, :], positions, 0.0, float(P), ALU.is_lt, ALU.mult), 1)
            setup_link(nc.vector.tensor_tensor(tmp_pos[:, 0, :], positions, tmp_pos[:, 1, :], ALU.add), 2)
            setup_link(nc.vector.tensor_scalar(tmp_pos[:, 1, :], tmp_pos[:, 0, :], 0.0, float(P - 1), ALU.max, ALU.min), 3)
            setup_link(nc.vector.tensor_scalar(tmp_pos[:, 0, :], tmp_pos[:, 1, :], row_number[:, 0:1], None, ALU.is_equal), 4)
            nc.vector.tensor_copy(tmp_pos[:, 1, :], tmp_pos[:, 0, :]).then_inc(s_onehot, 1)
            dve.wait_ge(s_rope_full, 1)
            nc.vector.tensor_copy(rope[:], values.banks[0][:, 0:32]).then_inc(s_rope, 1)
            dve.wait_ge(s_rope, 1)
            dve.wait_ge(s_set, 1)
            dve.wait_ge(s_tanh_gates, 1)

            with dve.Fori(0, ITERATIONS) as it:
                state["it"] = it
                state["n"] = 0

                def statistics(name, s):
                    n = norm_no[name, s]
                    nc.vector.bn_stats(moments[:, n, :], x[s][:])
                    dve.drain()
                    link(nc.vector.bn_aggr(mean_var[:, n, :], moments[:, n, :]))
                    mean, var = mean_var[:, n, 0:1], mean_var[:, n, 1:2]
                    if name not in CENTRED:
                        link(nc.vector.scalar_tensor_tensor(out=square[:, n:n + 1], in0=mean, scalar=mean, in1=var, op0=ALU.mult, op1=ALU.add))
                        var = square[:, n:n + 1]
                    nc.vector.tensor_scalar(var_eps[:, n:n + 1], var, EPS[name], None, ALU.add).then_inc(s_var, 1)

                def normalise(name, s):
                    n = norm_no[name, s]
                    dve.wait_ge(s_rstd, it * N_NORMS + n + 1)
                    r = rstd[:, n:n + 1]
                    if name == "fuse":
                        link(nc.vector.scalar_tensor_tensor(out=x[s][:], in0=x[s][:], scalar=r, in1=fuse_gain[:], op0=ALU.mult, op1=ALU.mult))
                    elif name == "self":
                        for v in range(2):
                            link(nc.vector.tensor_scalar(rstd_expert[:, s, v:v + 1], r, expert[s][:, v:v + 1], None, ALU.mult))
                        nc.vector.tensor_scalar(xn[s][:, 0, :], x[s][:], rstd_expert[:, s, 0:1], None, ALU.mult)
                        nc.vector.tensor_scalar(xn[s][:, 1, :], x[s][:], rstd_expert[:, s, 1:2], None, ALU.mult).then_inc(s_xn, 1)
                    elif name in CENTRED:
                        nc.vector.tensor_scalar(xn[s][:, 0, :], x[s][:], mean_var[:, n, 0:1], r, ALU.subtract, ALU.mult).then_inc(s_xn, 1)
                    else:
                        nc.vector.tensor_scalar(xn[s][:, 0, :], x[s][:], r, None, ALU.mult).then_inc(s_xn, 1)

                for kind, block, s, i in STEPS:
                    if kind == "mem":
                        dve.wait_ge(s_side[s], (it + 1) * 48)
                        nc.vector.tensor_scalar(keep[s][:], keep_in[s][:], 1.0, -MASKED, ALU.subtract, ALU.mult).then_inc(s_keep, 1)
                        link(nc.vector.tensor_scalar(expert[s][:, 2:4], types[s][:], 1.0, None, ALU.is_equal))
                        link(nc.vector.tensor_tensor(expert[s][:, 0:1], expert[s][:, 2:3], expert[s][:, 3:4], ALU.mult))
                        nc.vector.tensor_scalar(expert[s][:, 1:2], expert[s][:, 0:1], -1.0, 1.0, ALU.mult, ALU.add)

                    elif kind == "scores":
                        key = (block, s, i)
                        n = unit_no[key]
                        g = 1 if block == "fuse" else GROUP
                        scores.wait_full(dve, it, key)
                        nc.vector.tensor_reduce(minus_max[:, n, 0:g], scores.bank(key)[:, 0:g * P].rearrange("p (h k) -> p h k", h=g),
                                                AX.X, ALU.max, negate=True).then_inc(s_max, 1)

                    elif kind == "turn":
                        key = (block, s, i)
                        g = 1 if block == "fuse" else GROUP
                        turned.wait_full(dve, it, key)
                        values.wait_full_before(dve, it, key)
                        b = turned.of[key][0]
                        turned.empty(nc.vector.tensor_copy(probsT[b][:, 0:g, :], turned.bank(key)[:, 0:g * P].rearrange("p (h k) -> p h k", h=g)), key)

                    elif kind == "values":
                        key = (block, s, i)
                        n = unit_no[key]
                        g = 1 if block == "fuse" else GROUP
                        values.wait_full(dve, it, key)
                        link(nc.vector.reciprocal(inv_total[:, n, 0:g], total[:, n, 0:g]))
                        if block == "fuse":
                            ins = nc.vector.tensor_scalar(context[s], values.bank(key)[:, 0:D], inv_total[:, n, 0:1], None, ALU.mult)
                        else:
                            h = HEAD[block]
                            c = i * GROUP * h
                            ins = nc.vector.tensor_tensor(heads[s][:, c:c + GROUP * h].rearrange("p (g h) -> p g h", g=GROUP),
                                                          values.bank(key)[:, 0:GROUP * h].rearrange("p (g h) -> p g h", g=GROUP),
                                                          inv_total[:, n, :].unsqueeze(2).to_broadcast([P, GROUP, h]), ALU.mult)
                        values.empty(ins, key)

                    elif kind == "gate":
                        products.wait_emptied(dve, it, (kind, block, s, 0))
                        link(nc.vector.scalar_tensor_tensor(out=gated[s], in0=gate_tanh[s], scalar=1.0, in1=context[s], op0=ALU.add, op1=ALU.mult))
                        dve.wait_ge(s_x_free[s], it + 1)
                        link(nc.vector.scalar_tensor_tensor(out=x[s][:], in0=gated[s], scalar=0.5, in1=x_in[s][:], op0=ALU.mult, op1=ALU.add))

                    elif kind == "kv" and i % 2 == 0:
                        key = (kind, block, s, i)
                        products.wait_full(dve, it, key)
                        products.empty(nc.vector.tensor_tensor(
                            keys[s][:, i * 512:(i + 2) * 512].rearrange("p (c h n) -> p c h n", c=4, h=2),
                            products.bank(key)[:].rearrange("p (c n) -> p c n", c=4).unsqueeze(2).to_broadcast([P, 4, 2, P]),
                            member[:, 0:2].unsqueeze(1).unsqueeze(3).to_broadcast([P, 4, 2, P]), ALU.mult), key)

                    elif kind == "qkv" and i == 0:
                        key = (kind, block, s, 0)
                        products.wait_full(dve, it, key)
                        qk = products.bank(key)[:].rearrange("p (h r) -> p h r", r=16)
                        ra, rb = (t[s].rearrange("p (h r) -> p h r", r=16) for t in (rope_a, rope_b))
                        nc.vector.tensor_tensor(ra, qk, rope[:, 0:16].unsqueeze(1).to_broadcast([P, 32, 16]), ALU.mult)
                        nc.vector.tensor_tensor(rb[:, :, 0:8], qk[:, :, 8:16], rope[:, 16:24].unsqueeze(1).to_broadcast([P, 32, 8]), ALU.mult)
                        ins = nc.vector.tensor_tensor(rb[:, :, 8:16], qk[:, :, 0:8], rope[:, 24:32].unsqueeze(1).to_broadcast([P, 32, 8]), ALU.mult)
                        products.empty(ins, key)
                        products.wait_emptied(dve, it, key)
                        nc.vector.tensor_tensor(roped[s], rope_a[s], rope_b[s], ALU.add).then_inc(s_roped, 1)

                    elif kind == "qkv":
                        key = (kind, block, s, 1)
                        products.wait_full(dve, it, key)
                        products.empty(nc.vector.tensor_copy(vals[s][:, 0:D], products.bank(key)[:, 0:D]), key)

                    elif kind == "qkT" and i == 1:
                        key = (kind, block, s, 1)
                        products.wait_full(dve, it, key)
                        for c in range(DC):
                            ins = nc.vector.tensor_tensor(
                                keys[s][:, c * 1024:(c + 1) * 1024].rearrange("p (h n) -> p h n", h=8),
                                products.bank(key)[:, c * P:(c + 1) * P].unsqueeze(1).to_broadcast([P, 8, P]),
                                member[:, 2:10].unsqueeze(2).to_broadcast([P, 8, P]), ALU.mult)
                        products.empty(ins, key)

                    elif kind == "cqk":
                        key = (kind, block, s, 0)
                        products.wait_full(dve, it, key)
                        bank = products.bank(key)
                        nc.vector.tensor_scalar(queries[s][:, 0:P], bank[:, 0:P], HEAD[block] ** -0.5, None, ALU.mult)
                        nc.vector.tensor_copy(vals[s][:, 0:P], bank[:, 2 * P:3 * P])
                        products.empty(nc.vector.tensor_tensor(
                            keys[s][:].rearrange("p (h n) -> p h n", h=16), bank[:, P:2 * P].unsqueeze(1).to_broadcast([P, 16, P]),
                            member[:, 10:26].unsqueeze(2).to_broadcast([P, 16, P]), ALU.mult), key)

                    elif kind in ("wo", "ff2", "down"):
                        key = (kind, block, s, 0)
                        products.wait_full(dve, it, key)
                        bank = products.bank(key)
                        if block in ("one", "three"):
                            g = GATES.index(block + ("_ff" if kind == "ff2" else ""))
                            ins = nc.vector.scalar_tensor_tensor(out=x[s][:], in0=bank[:, 0:D], scalar=tanh_gates[:, g:g + 1], in1=x[s][:],
                                                                 op0=ALU.mult, op1=ALU.add)
                        elif block == "cross":
                            ins = nc.vector.tensor_tensor(x[s][:], bank[:, 0:D], x[s][:], ALU.add)
                        else:
                            link(nc.vector.scalar_tensor_tensor(out=x[s][:], in0=bank[:, 0:D], scalar=expert[s][:, 0:1], in1=x[s][:],
                                                                op0=ALU.mult, op1=ALU.add))
                            ins = nc.vector.scalar_tensor_tensor(out=x[s][:], in0=bank[:, D:2 * D], scalar=expert[s][:, 1:2], in1=x[s][:],
                                                                 op0=ALU.mult, op1=ALU.add)
                        products.empty(ins, key)
                        if (kind, block) in STATISTICS:
                            products.wait_emptied(dve, it, key)

                    elif kind == "xn":
                        normalise(block, s)

                    elif kind == "gu":
                        key = (kind, block, s, i)
                        dve.wait_ge(s_silu, it * len(gu_no) + gu_no[s, i] + 1)
                        e, pair = i // (FC // 2), i % (FC // 2)
                        products.empty(nc.vector.tensor_tensor(hidden2[s][:, e, 2 * pair:2 * pair + 2, :],
                                                               products.bank(key)[:, D:2 * D].rearrange("p (c n) -> p c n", c=2),
                                                               silu[s][i % 2].rearrange("p (c n) -> p c n", c=2), ALU.mult), key)
                    if (kind, block) in STATISTICS:
                        statistics(STATISTICS[kind, block], s)
                assert state["n"] == N_LINKS, (state["n"], N_LINKS)


def kernel(**inputs):
    import numpy as _np
    import concourse.bacc as _bacc
    from concourse import mybir as _mybir
    from concourse.bass_utils import run_bass_kernel_spmd as _run

    a = {name: _np.asarray(v) for name, v in inputs.items()}

    def by_chunk(m):
        return m.reshape(-1, P, m.shape[1]).transpose(1, 0, 2)

    L0, L1, L2, L3 = (f"L{i}_xattn_" for i in range(4))
    full = (FC - 1) * P
    arrays = {
        "x": a["x"],
        "xT": a["x"].reshape(BATCH, P, DC, P).transpose(0, 3, 2, 1),
        "ctxT": a["ctx_1024"].transpose(0, 2, 1),
        "keep": a["mask_BxS2_bk0"],
        "types": _np.stack([a["mask_BxS_ik0"], _np.pad(a["mask_BxS_ik0"][:, 1:], ((0, 0), (0, 1)))], axis=2),
        "positions": a["pos_1xS"],
        "mem": a[L0 + "W_mem"].T, "gate": by_chunk(a[L0 + "W_gate"].T),
        "gate_bias": a[L0 + "b_gate"][None], "fuse_gain": a[L0 + "norm_w"][None],
        "gates": _np.concatenate([a[L1 + "attn_gate"], a[L1 + "ff_gate"], a[L3 + "attn_gate"], a[L3 + "ff_gate"]])[None],
        "v_qkv": by_chunk(a[L2 + "v_qkv"]), "l_qkv": by_chunk(a[L2 + "l_qkv"]),
        "vl_dense": by_chunk(_np.concatenate([a[L2 + "v_dense"], a[L2 + "l_dense"]], axis=1)),
        "cq": by_chunk(a[L2 + "cq_w"]), "ckv": a[L2 + "ckv_w"], "cdense": a[L2 + "cdense_w"],
    }
    for name, pre in (("one", L1), ("three", L3)):
        arrays[name + "_q"] = by_chunk(a[pre + "Wq"])
        arrays[name + "_kv"] = a[pre + "Wkv"]
        arrays[name + "_o"] = by_chunk(a[pre + "Wo"])
        arrays[name + "_1"] = by_chunk(a[pre + "W1"])
        arrays[name + "_2"] = by_chunk(a[pre + "W2"])
    for e in "vl":
        arrays[e + "_gate"], arrays[e + "_up"] = by_chunk(a[L2 + e + "_gate"]), by_chunk(a[L2 + e + "_up"])
        arrays[e + "_down0"], arrays[e + "_down1"] = by_chunk(a[L2 + e + "_down"][:full]), a[L2 + e + "_down"][full:]
    gains = [(L1 + "ln_q_g", L1 + "ln_q_b"), (L1 + "ln_ff_g", L1 + "ln_ff_b"), (L2 + "ln_in_w",) * 2, (L2 + "ln_post_cross_w",) * 2,
             (L2 + "ln_post_attn_w",) * 2, (L3 + "ln_q_g", L3 + "ln_q_b"), (L3 + "ln_ff_g", L3 + "ln_ff_b")]
    arrays["features"] = _np.stack([_np.stack([a[n].reshape(DC, P) for n in pair]) for pair in gains]).transpose(3, 0, 1, 2)
    arrays["ident"] = _np.eye(P, dtype=_np.float32)
    rows = _np.arange(P)
    arrays["member"] = _np.concatenate([(rows[:, None] // w == _np.arange(P // w)) for w in (64, 16, 8)], axis=1).astype(_np.float32)
    arrays["row_number"] = rows[:, None].astype(_np.float32)
    arrays["causal"] = _np.where(rows[:, None] >= rows, 0.0, MASKED).astype(_np.float32)
    inverse = (1.0 / 10000.0 ** (_np.arange(0, 16, 2, dtype=_np.float32) / 16)).astype(_np.float32)
    angle = rows[:, None].astype(_np.float32) * inverse
    arrays["rope_rows"] = _np.concatenate([_np.cos(angle), _np.cos(angle), -_np.sin(angle), _np.sin(angle)], axis=1).astype(_np.float32)

    nc = _bacc.Bacc("TRN2", target_bir_lowering=False, num_devices=1)
    given, aps = {}, {}
    for name, v in arrays.items():
        given["in_" + name] = _np.ascontiguousarray(v)
        aps[name] = nc.dram_tensor("in_" + name, v.shape, _mybir.dt.from_np(v.dtype), kind="ExternalInput").ap()
    for e in "vl":
        aps[e + "_down"] = (aps[e + "_down0"], aps[e + "_down1"])
    out = nc.dram_tensor("out", a["x"].shape, _mybir.dt.float32, kind="ExternalOutput").ap()
    build(nc, aps, out)
    r = _run(nc, [given], core_ids=[0])
    return r.results[0]["out"]
```

```python
from contextlib import ExitStack

import concourse.bass as bass
from concourse import mybir

F32 = mybir.dt.float32
BF16 = mybir.dt.bfloat16
I32 = mybir.dt.int32
U8 = mybir.dt.uint8
ALU = mybir.AluOpType
ACT = mybir.ActivationFunctionType
AX = mybir.AxisListType

P = 128
BATCH = 8
SLOTS = 2
ITERATIONS = BATCH // SLOTS
D = 256
DC = D // P
INNER = 1024
IC = INNER // P
FF = 688
FFULL = FF // P
FREST = FF - FFULL * P
FC = 1 + 2 * FFULL
HEADS = 16
GROUP = 4
UNITS = HEADS // GROUP
HEAD = {"one": 64, "self": 16, "cross": 8, "three": 64}
MASKED = -(2.0 ** 127)
EPS = {"fuse": 1e-6, "one": 1e-5, "one_ff": 1e-5, "self": 1e-6, "cross": 1e-6, "mlp": 1e-6,
       "three": 1e-5, "three_ff": 1e-5}
FEATURES = ["one", "one_ff", "self", "cross", "mlp", "three", "three_ff"]
GATES = ["one", "one_ff", "three", "three_ff"]
STATISTICS = {("gate", None): "fuse", ("xn", "fuse"): "one", ("wo", "one"): "one_ff", ("ff2", "one"): "self",
              ("wo", "self"): "cross", ("wo", "cross"): "mlp", ("down", "mlp"): "three", ("wo", "three"): "three_ff"}
CENTRED = ("one", "one_ff", "three", "three_ff")
LINKS = {("mem", None): 2, ("gate", None): 2, ("xn", "fuse"): 1, ("xn", "self"): 2, ("wo", "self"): 1, ("down", "mlp"): 1}
VALUES_LINKS = 1
STATISTICS_LINKS = {True: 1, False: 2}


ORDER = """
mem:A0 mem:B0 scores.fuse:A0 kv.one:B3v scores.fuse:B0 kv.one:A1s turn.fuse:A0v turn.fuse:B0v values.fuse:A0
kv.one:A2v mcT:A0 values.fuse:B0 gate:A0 mcT:B0 kv.one:B1v xn.fuse:A0 kv.one:B0s kv.one:A3s kv.one:A0s xn.one:A0
gate:B0 nT.one:A0s kv.one:B2s q.one:A0s q.one:A1s xn.fuse:B0 xn.one:B0 scores.one:A0 nT.one:B0v scores.one:A1
q.one:B0v turn.one:A0s scores.one:A2 turn.one:A1v values.one:A0 scores.one:A3 values.one:A1 turn.one:A2v
q.one:B1v turn.one:A3v values.one:A2 oT.one:A0v values.one:A3 scores.one:B0 scores.one:B1 oT.one:A1v wo.one:A0
turn.one:B0s turn.one:B1s scores.one:B2 xn.one_ff:A0 values.one:B0 values.one:B1 nT.one_ff:A0v scores.one:B3
turn.one:B2v oT.one:B0v ff1.one:A0 values.one:B2 turn.one:B3v ff1.one:A1 values.one:B3 ff2.one:A0 xn.self:A0
oT.one:B1s wo.one:B0 xn.one_ff:B0 nT.self:A0s qkv.self:A0 nT.one_ff:B0s qkv.self:A1v ff1.one:B0 qkT.self:A1
qkT.self:A0s ff1.one:B1 scores.self:A0 qkT.self:A2 ff2.one:B0 turn.self:A0s scores.self:A1 xn.self:B0
values.self:A0 scores.self:A2 nT.self:B0v turn.self:A1s scores.self:A3 ckv.cross:A0 qkv.self:B0 turn.self:A2s
values.self:A1 qkv.self:B1s turn.self:A3s qkT.self:B0s qkT.self:B1 values.self:A2 values.self:A3 scores.self:B0
oT.self:A0v scores.self:B1 qkT.self:B2 wo.self:A0 turn.self:B0s ckv.cross:A1s scores.self:B2 turn.self:B1v
xn.cross:A0 scores.self:B3 values.self:B0 nT.cross:A0v values.self:B1 ckv.cross:B0 turn.self:B2s cq.cross:A0s
turn.self:B3s values.self:B2 values.self:B3 scores.cross:A0 oT.self:B0v ckv.cross:B1v scores.cross:A1 wo.self:B0
turn.cross:A0s turn.cross:A1s scores.cross:A2 xn.cross:B0 values.cross:A0 scores.cross:A3 nT.cross:B0v
values.cross:A1 turn.cross:A2s cq.cross:B0v scores.cross:B0 turn.cross:A3v scores.cross:B1 values.cross:A2
values.cross:A3 turn.cross:B0s scores.cross:B2 oT.cross:A0v turn.cross:B1s scores.cross:B3 values.cross:B0
wo.cross:A0 kv.three:A3s values.cross:B1 turn.cross:B2s kv.three:A1s xn.mlp:A0 turn.cross:B3v nT.mlp:A0s
values.cross:B2 values.cross:B3 gu.mlp:A0 oT.cross:B0s gu.mlp:A1 wo.cross:B0 gu.mlp:A2 xn.mlp:B0 kv.three:B1s
gu.mlp:A3 nT.mlp:B0s gu.mlp:A4 gu.mlp:A5 gu.mlp:B0 down.mlp:A0 gu.mlp:B1 xn.three:A0 kv.three:A2v gu.mlp:B2
nT.three:A0v gu.mlp:B3 kv.three:A0s gu.mlp:B4 q.three:A0v gu.mlp:B5 kv.three:B3v scores.three:A0 down.mlp:B0
q.three:A1s turn.three:A0v xn.three:B0 scores.three:A1 kv.three:B2s scores.three:A2 nT.three:B0v kv.three:B0v
values.three:A0 turn.three:A1s scores.three:A3 q.three:B0s turn.three:A2s values.three:A1 q.three:B1v
scores.three:B0 turn.three:A3v scores.three:B1 values.three:A2 oT.three:A0s values.three:A3 turn.three:B0v
scores.three:B2 turn.three:B1v values.three:B0 scores.three:B3 values.three:B1 oT.three:A1v turn.three:B2s
wo.three:A0 turn.three:B3s values.three:B2 values.three:B3 xn.three_ff:A0 oT.three:B0s oT.three:B1s
nT.three_ff:A0v wo.three:B0 xn.three_ff:B0 ff1.three:A0 ff1.three:A1 nT.three_ff:B0v ff2.three:A0 ff1.three:B0
ff1.three:B1 ff2.three:B0
"""


def steps():
    out = []
    for word in ORDER.split():
        what, where = word.split(":")
        kind, _, block = what.partition(".")
        out.append((kind, block or None, "AB".index(where[0]), int(where[1])))
    return out


COPIED_BY = {step: word[-1] for step, word in zip(steps(), ORDER.split()) if word[-1] in "sv"}



class Pool:

    def __init__(self, banks, full, emptied):
        self.banks, self.full, self.emptied = banks, full, emptied
        self.uses = [0] * len(banks)
        self.of = {}
        self.n = 0
        self.waited = {}

    def plan(self, key):
        b = self.n % len(self.banks)
        self.of[key] = (b, self.uses[b])
        self.uses[b] += 1
        self.n += 1

    def bank(self, key):
        return self.banks[self.of[key][0]]

    def wait_before(self, eng, it, key):
        b, k = self.of[key]
        self.waited[b] = k
        eng.wait_ge(self.emptied[b], it * self.uses[b] + k + 1)

    def wait_full(self, eng, it, key):
        b, k = self.of[key]
        eng.wait_ge(self.full[b], it * self.uses[b] + k + 2)

    def wait_emptied(self, eng, it, key):
        b, k = self.of[key]
        eng.wait_ge(self.emptied[b], it * self.uses[b] + k + 2)

    def wait_copied(self, pe, it, *keys):
        last = {}
        for key in keys:
            b, k = self.of[key]
            if k >= max(self.waited.get(b, 0), self.of[last[b]][1] if b in last else 0):
                last[b] = key
        for b, key in last.items():
            self.wait_emptied(pe, it, key)
            self.waited[b] = self.of[key][1] + 1

    def filled(self, ins, key):
        ins.then_inc(self.full[self.of[key][0]], 1)

    def empty(self, ins, key):
        ins.then_inc(self.emptied[self.of[key][0]], 1)


def build(nc, a, out):
    STEPS = steps()
    with ExitStack() as ctx:
        def sb(name, shape, dt=F32):
            return ctx.enter_context(nc.sbuf_tensor(name, shape, dt))

        def sem(name):
            return ctx.enter_context(nc.semaphore(name))

        w = {name: sb("w_" + name, shape) for name, shape in {
            "mem": [P, D], "gate": [P, 2 * DC, D],
            "one_q": [P, DC, INNER], "one_kv": [P, 2 * INNER], "one_o": [P, IC, D],
            "one_1": [P, DC, INNER], "one_2": [P, IC, D],
            "v_qkv": [P, DC, 3 * D], "l_qkv": [P, DC, 3 * D], "vl_dense": [P, DC, 2 * D],
            "cq": [P, DC, P], "ckv": [P, 2 * P], "cdense": [P, D],
            "mlp_gate": [P, DC, FC * P], "mlp_up": [P, DC, FC * P], "down_rest": [P, 2 * D], "down": [P, 2 * FFULL, D],
            "three_q": [P, DC, INNER], "three_kv": [P, 2 * INNER], "three_o": [P, IC, D],
            "three_1": [P, DC, INNER], "three_2": [P, IC, D]}.items()}
        gates = sb("gates", [P, len(GATES)])
        tanh_gates = sb("tanh_gates", [P, len(GATES)])
        fuse_gain = sb("fuse_gain", [P, D])
        gate_bias = sb("gate_bias", [P, D])
        bias_parts = sb("bias_parts", [P, D], BF16)
        ones_bf = sb("ones_bf", [P, P], BF16)
        minus_half = sb("minus_half", [P, 1])
        n_features, n_member = len(FEATURES) * 2 * DC, 2 + 8 + 16
        table = sb("table", [P, n_features + P + n_member + 1])
        features = table[:, 0:n_features].rearrange("p (f g c) -> p f g c", g=2, c=DC)
        ident = table[:, n_features:n_features + P]
        member = table[:, n_features + P:n_features + P + n_member]
        row_number = table[:, n_features + P + n_member:]
        ident_bf = sb("ident_bf", [P, P], BF16)
        causal = sb("causal", [P, P], BF16)
        rope = sb("rope", [P, 32])

        slots = range(SLOTS)
        x_in = [sb(f"x_in{s}", [P, D]) for s in slots]
        x_inT = [sb(f"x_inT{s}", [P, DC, P]) for s in slots]
        ctxT = [sb(f"ctxT{s}", [P, P]) for s in slots]
        keep_in = [sb(f"keep_in{s}", [1, P], U8) for s in slots]
        keep = [sb(f"keep{s}", [1, P], BF16) for s in slots]
        types = [sb(f"types{s}", [P, 2], I32) for s in slots]
        expert = [sb(f"expert{s}", [P, 4]) for s in slots]
        x = [sb(f"x{s}", [P, D]) for s in slots]
        xnT = [sb(f"xnT{s}", [P, DC, 2, P]) for s in slots]
        keys = [sb(f"keys{s}", [P, 2048]) for s in slots]
        queries = [sb(f"queries{s}", [P, INNER]) for s in slots]
        vals = [sb(f"vals{s}", [P, INNER]) for s in slots]
        heads = [sb(f"heads{s}", [P, INNER]) for s in slots]
        xn = [heads[s][:, 0:2 * D].rearrange("p (v d) -> p v d", v=2) for s in slots]
        context = [heads[s][:, 2 * D:3 * D] for s in slots]
        contextT = [queries[s][:, 0:DC * P].rearrange("p (c n) -> p c n", c=DC) for s in slots]
        memT = [heads[s][:, 0:DC * P].rearrange("p (c n) -> p c n", c=DC) for s in slots]
        mem = [heads[s][:, D:2 * D] for s in slots]
        gate_tanh = [queries[s][:, D:2 * D] for s in slots]
        gated = [queries[s][:, 2 * D:3 * D] for s in slots]
        hidden = [keys[s][:, 0:INNER].rearrange("p (c n) -> p c n", c=IC) for s in slots]
        hidden2 = [keys[s][:, 0:FC * P].rearrange("p (c n) -> p c n", c=FC) for s in slots]
        roped = [heads[s][:, 0:2 * D] for s in slots]
        rope_a = [heads[s][:, 0:2 * D] for s in slots]
        rope_b = [heads[s][:, 2 * D:4 * D] for s in slots]
        silu = [[heads[s][:, D * b:D * b + D] for b in range(4)] for s in slots]
        probs = [sb(f"probs{i}", [P, GROUP, P]) for i in range(2)]
        probsT = [sb(f"probsT{i}", [P, GROUP, P]) for i in range(2)]

        masks_in = probs[1][:].rearrange("p g n -> p (g n)")[:, 0:P + 32]
        causal_f = masks_in[:, 0:P]
        positions = probs[0][:, 1, :].bitcast(I32)
        tmp_pos = probs[0][:, 2:4, :]
        rope_rows = masks_in[:, P:P + 32]

        def psum_pool(name, n):
            return Pool([ctx.enter_context(nc.psum_tensor(f"{name}{b}", [P, 512], F32)) for b in range(n)],
                        [sem(f"{name}_full{b}") for b in range(n)], [sem(f"{name}_emptied{b}") for b in range(n)])

        products, scores, attended = psum_pool("products", 4), psum_pool("scores", 2), psum_pool("attended", 2)

        unit_no, norm_no, xn_no, roped_no, gu_no = {}, {}, {}, {}, {}
        for kind, block, s, i in STEPS:
            if kind == "scores":
                unit_no[block, s, i] = len(unit_no)
                scores.plan((block, s, i))
            elif kind == "turn":
                attended.plan(("turn", block, s, i))
            elif kind == "values":
                attended.plan(("values", block, s, i))
            elif kind == "xn":
                if block != "fuse":
                    xn_no[block, s] = len(xn_no)
            else:
                products.plan((kind, block, s, i))
                if (kind, i) == ("qkv", 0):
                    roped_no[s] = len(roped_no)
                if kind == "gu":
                    gu_no[s, i] = len(gu_no)
            if (kind, block) in STATISTICS:
                norm_no[STATISTICS[kind, block], s] = len(norm_no)
        N_UNITS, N_NORMS = len(unit_no), len(norm_no)
        N_LINKS = 0
        for kind, block, s, i in STEPS:
            N_LINKS += LINKS.get((kind, block), 0) + VALUES_LINKS * (kind == "values")
            if (kind, block) in STATISTICS:
                N_LINKS += STATISTICS_LINKS[STATISTICS[kind, block] in CENTRED]

        def still_to_come(kind, other, unit):
            n = unit_no[unit]
            before = [key for key, m in unit_no.items() if m == n - 2]
            return [(other, *key) for key in before if STEPS.index((other, *key)) > STEPS.index((kind, *unit))]

        moments = sb("moments", [P, N_NORMS, 6])
        mean_var = sb("mean_var", [P, N_NORMS, 2])
        square = sb("square", [P, N_NORMS])
        var_eps = sb("var_eps", [P, N_NORMS])
        rstd = sb("rstd", [P, N_NORMS])
        rstd_expert = sb("rstd_expert", [P, SLOTS, 2])
        minus_max = sb("minus_max", [P, N_UNITS, GROUP])
        total = sb("total", [P, N_UNITS, GROUP])
        inv_total = sb("inv_total", [P, N_UNITS, GROUP])

        s_weights = {g: sem("weights_loaded_" + g) for g in ("memory", "fuse", "one_kv", "one", "one_ff", "two_a", "two_mlp", "three")}
        n_weights = dict.fromkeys(s_weights, 0)
        s_tables = sem("tables_loaded")
        s_consts = sem("constants_loaded")
        s_bias = sem("gate_bias_split")
        s_set = sem("constants_set")
        s_onehot = sem("positions_one_hot")
        s_rope_full = sem("rope_rows_gathered")
        s_rope = sem("rope_ready")
        s_tanh_gates = sem("tanh_gates_ready")
        s_x = [sem(f"x_loaded{s}") for s in slots]
        s_side = [sem(f"side_inputs_loaded{s}") for s in slots]
        s_x_used = [sem(f"x_input_used{s}") for s in slots]
        s_side_used = [sem(f"side_inputs_used{s}") for s in slots]
        s_keep = sem("key_masks_ready")
        s_link = sem("vector_done")
        s_var = sem("variance_ready")
        s_rstd = sem("rstd_ready")
        s_xn = sem("normalised_ready")
        s_max = sem("minus_max_ready")
        s_roped = sem("roped_ready")
        s_silu = sem("silu_ready")
        s_stored = [sem(f"result_stored{s}") for s in slots]
        s_x_free = [sem(f"x_free{s}") for s in slots]

        block_ = ctx.enter_context(nc.Block())

        WEIGHTS = [("memory", "mem"), ("one_kv", "one_kv"), ("fuse", "gate"), ("one", "one_q"), ("one", "one_o"),
                   ("one_ff", "one_1"), ("one_ff", "one_2"), ("two_a", "v_qkv"), ("two_a", "l_qkv"),
                   ("two_a", "vl_dense"), ("two_a", "cq"), ("two_a", "ckv"), ("two_a", "cdense"),
                   ("two_mlp", "mlp_gate"), ("two_mlp", "mlp_up"), ("two_mlp", "down_rest"), ("two_mlp", "down"), ("three", "three_kv"), ("three", "three_q"),
                   ("three", "three_o"), ("three", "three_1"), ("three", "three_2")]
        for group, name in WEIGHTS:
            n_weights[group] += 16
        TABLES = [(positions, a["positions"].partition_broadcast(P)), (table[:], a["table"]), (masks_in, a["causal_rope"])]
        CONSTS = [(gates[:], a["gates"].partition_broadcast(P)), (fuse_gain[:], a["fuse_gain"].partition_broadcast(P)),
                  (gate_bias[:], a["gate_bias"])]

        def load_weight(sp, group, name):
            sp.dma_start(w[name][:], a[name]).then_inc(s_weights[group], 16)

        def copy_out(eng, it, kind, block, s, i):
            def scaled(out, in_, scale=1.0, offset=None):
                if eng is nc.scalar:
                    if offset is None:
                        return nc.scalar.activation(out, in_, ACT.Copy, scale=scale)
                    return nc.scalar.activation(out, in_, ACT.Identity, scale=scale, bias=offset)
                if offset is not None:
                    return nc.vector.tensor_scalar(out, in_, scale, offset, ALU.mult, ALU.add)
                if scale == 1.0:
                    return nc.vector.tensor_copy(out, in_)
                return nc.vector.tensor_scalar(out, in_, scale, None, ALU.mult)

            key = (kind, block, s, i)
            if kind == "turn":
                attended.wait_full(eng, it, key)
                for before in still_to_come("turn", "values", key[1:]):
                    attended.wait_full(eng, it, before)
                n = (1 if block == "fuse" else GROUP) * P
                attended.empty(scaled(probsT[unit_no[block, s, i] % 2][:].rearrange("p g n -> p (g n)")[:, 0:n],
                                      attended.bank(key)[:, 0:n]), key)
                return

            products.wait_full(eng, it, key)
            bank = products.bank(key)
            if kind == "kv" and i % 2 == 0:
                out = keys[s][:, i * 512:(i + 2) * 512].rearrange("p (c h n) -> p c h n", c=4, h=2)
                by_chunk = bank[:].rearrange("p (c n) -> p c n", c=4)
                if eng is nc.scalar:
                    for h in range(2):
                        ins = scaled(out[:, :, h, :], by_chunk, member[:, h:h + 1])
                else:
                    ins = nc.vector.tensor_tensor(out, by_chunk.unsqueeze(2).to_broadcast([P, 4, 2, P]),
                                                  member[:, 0:2].unsqueeze(1).unsqueeze(3).to_broadcast([P, 4, 2, P]), ALU.mult)
            elif kind == "kv":
                ins = scaled(vals[s][:, (i // 2) * 512:(i // 2 + 1) * 512], bank[:])
            elif kind == "nT":
                nv = 2 if block == "self" else 1
                f = FEATURES.index(block)
                for c in range(DC):
                    ins = scaled(xnT[s][:, c, 0:nv, :], bank[:, c * nv * P:(c + 1) * nv * P].rearrange("p (v n) -> p v n", v=nv),
                                 features[:, f, 0, c:c + 1], features[:, f, 1, c:c + 1] if block in CENTRED else None)
            elif kind == "q":
                ins = scaled(queries[s][:, i * 512:(i + 1) * 512], bank[:], HEAD[block] ** -0.5)
            elif kind == "qkT":
                ins = scaled(queries[s][:, 0:D], bank[:, 0:D], HEAD[block] ** -0.5)
            elif kind == "qkv":
                ins = scaled(vals[s][:, 0:D], bank[:, 0:D])
            elif kind == "ckv":
                ins = scaled(vals[s][:, 0:P], bank[:, 0:P])
            elif kind == "cq":
                ins = scaled(queries[s][:, 0:P], bank[:, 0:P], HEAD[block] ** -0.5)
            else:
                n = min(HEAD[block] * HEADS // P, 4) * P
                ins = scaled(queries[s][:, i * 512:i * 512 + n], bank[:, 0:n])
            products.empty(ins, key)

        @block_.sync
        def _(sp):
            def load_x(it, s):
                sp.wait_ge(s_x_used[s], it + 1)
                b = it * SLOTS + s
                sp.dma_start(x_in[s][:], a["x"][bass.ds(b, 1), :, :].rearrange("o p n -> p (o n)")).then_inc(s_x[s], 16)
                sp.dma_start(x_inT[s][:], a["xT"][bass.ds(b, 1), :, :, :].rearrange("o p c n -> p (o c) n")).then_inc(s_x[s], 16)

            def load_side(it, s):
                sp.wait_ge(s_side_used[s], it + 1)
                b = it * SLOTS + s
                sp.dma_start(ctxT[s][:], a["ctxT"][bass.ds(b, 1), :, :].rearrange("o p n -> p (o n)")).then_inc(s_side[s], 16)
                sp.dma_start(keep_in[s][:], a["keep"][bass.ds(b, 1), :]).then_inc(s_side[s], 16)
                sp.dma_start(types[s][:], a["types"][bass.ds(b, 1), :, :].rearrange("o p n -> p (o n)")).then_inc(s_side[s], 16)

            load_weight(sp, *WEIGHTS[0])
            for s in slots:
                load_side(0, s)
            for s in slots:
                load_x(0, s)
            for group, name in WEIGHTS[1:]:
                load_weight(sp, group, name)

            with sp.Fori(1, ITERATIONS) as it:
                for s in slots:
                    load_x(it, s)
                for s in slots:
                    load_side(it, s)

        @block_.gpsimd
        def _(pool):
            for p in (products, scores, attended):
                for q in (*p.full, *p.emptied):
                    pool.sem_inc(q, 1)
            for q in (*s_x_used, *s_side_used, *s_x_free):
                pool.sem_inc(q, 1)
            nc.gpsimd.memset(minus_half[:], -0.5).then_inc(s_set, 1)
            pool.wait_ge(s_set, 1)

            pool.wait_ge(s_consts, 16 * len(CONSTS))
            rest = heads[1][:, 3 * D:4 * D]
            low = slice(64, 96)
            nc.gpsimd.tensor_copy(bias_parts[:], gate_bias[:]).then_inc(s_bias, 1)
            pool.wait_ge(s_bias, 1)
            nc.gpsimd.tensor_tensor(rest, gate_bias[:], bias_parts[:], ALU.subtract).then_inc(s_bias, 1)
            pool.wait_ge(s_bias, 2)
            nc.gpsimd.tensor_copy(bias_parts[32:64, :], rest[32:64, :]).then_inc(s_bias, 1)
            nc.gpsimd.tensor_copy(bias_parts[low, :], rest[low, :]).then_inc(s_bias, 1)
            pool.wait_ge(s_bias, 4)
            nc.gpsimd.tensor_tensor(rest[low, :], rest[low, :], bias_parts[low, :], ALU.subtract).then_inc(s_bias, 1)
            pool.wait_ge(s_bias, 5)
            nc.gpsimd.tensor_copy(bias_parts[low, :], rest[low, :]).then_inc(s_bias, 1)

            with pool.Fori(0, ITERATIONS) as it:
                for kind, block, s, _ in STEPS:
                    if (kind, block) in STATISTICS:
                        n = norm_no[STATISTICS[kind, block], s]
                        pool.wait_ge(s_var, it * N_NORMS + n + 1)
                        nc.gpsimd.tensor_tensor(rstd[:, n:n + 1], var_eps[:, n:n + 1], minus_half[:],
                                                ALU.pow).then_inc(s_rstd, 1)
                    if kind == "ff2" and block == "three":
                        pool.wait_ge(s_set, 1)
                        products.wait_emptied(pool, it, (kind, block, s, 0))
                        b = it * SLOTS + s
                        pool.dma_start(out[bass.ds(b, 1), :, :].rearrange("o p n -> p (o n)"), x[s][:]).then_inc(s_stored[s], 16)
                        pool.wait_ge(s_stored[s], (it + 1) * 16)
                        pool.sem_inc(s_x_free[s], 1)

        @block_.tensor
        def _(pe):
            mm = nc.tensor.matmul

            def have(group):
                pe.wait_ge(s_weights[group], n_weights[group])

            pe.wait_ge(s_onehot, 1)
            mm(attended.banks[0][:, 0:32], tmp_pos[:, 1, :], rope_rows, start=True, stop=True).then_inc(s_rope_full, 1)
            pe.wait_ge(s_rope, 1)

            with pe.Fori(0, ITERATIONS) as it:
                def fill(kind, block, s, i):
                    key = (kind, block, s, i)
                    products.wait_before(pe, it, key)
                    return key, products.bank(key)

                def copied(*sources):
                    products.wait_copied(pe, it, *sources)

                for kind, block, s, i in STEPS:
                    if kind == "mem":
                        pe.wait_ge(s_side[s], (it + 1) * 48)
                        have("memory")
                        key, bank = fill(kind, block, s, 0)
                        for c in range(DC):
                            mm(bank[:, c * P:(c + 1) * P], w["mem"][:, c * P:(c + 1) * P], ctxT[s][:], start=True, stop=True)
                        products.filled(mm(bank[:, D:2 * D], ctxT[s][:], w["mem"][:], start=True, stop=True), key)

                    elif kind == "scores":
                        key = (block, s, i)
                        scores.wait_before(pe, it, key)
                        bank = scores.bank(key)
                        u = i
                        if block == "fuse":
                            pe.wait_ge(s_x[s], (it + 1) * 32)
                            copied(("mem", None, s, 0))
                            for c in range(DC):
                                last = mm(bank[:, 0:P], x_inT[s][:, c, :], memT[s][:, c, :], start=(c == 0), stop=(c == DC - 1))
                        elif block == "self":
                            if u == 0:
                                copied(("qkT", block, s, 0), ("qkv", block, s, 1))
                            if u % 2 == 0:
                                copied(("qkT", block, s, 1 + u // 2))
                            mm(bank[:], ident_bf[:], causal[:].unsqueeze(1).to_broadcast([P, GROUP, P]), start=True, stop=False)
                            t = u // 2
                            last = mm(bank[:], queries[s][:, t * P:(t + 1) * P],
                                      keys[s][:, u * 512:(u + 1) * 512], start=False, stop=True)
                        elif block == "cross":
                            if u == 0:
                                copied(("cq", block, s, 0), ("ckv", block, s, 0), ("ckv", block, s, 1))
                            last = mm(bank[:], queries[s][:, 0:P], keys[s][:, u * 512:(u + 1) * 512], start=True, stop=True)
                        else:
                            if u == 0:
                                copied(("kv", block, s, 3), ("kv", block, s, 2), ("kv", block, s, 1), ("kv", block, s, 0))
                                pe.wait_ge(s_keep, it * SLOTS + s + 1)
                            if u % 2 == 0:
                                copied(("q", block, s, u // 2))
                            mm(bank[:], ones_bf[0:1, :], keep[s][:].unsqueeze(1).to_broadcast([1, GROUP, P]), start=True, stop=False)
                            for j in range(2):
                                t = 2 * u + j
                                last = mm(bank[:, j * 256:(j + 1) * 256], queries[s][:, t * P:(t + 1) * P],
                                          keys[s][:, t * 256:(t + 1) * 256], start=False, stop=(j == 1))
                        scores.filled(last, key)

                    elif kind == "turn":
                        key = ("turn", block, s, i)
                        attended.wait_before(pe, it, key)
                        scores.wait_emptied(pe, it, (block, s, i))
                        b = unit_no[block, s, i] % 2
                        for j in range(1 if block == "fuse" else GROUP):
                            last = nc.tensor.transpose(attended.bank(key)[:, j * P:(j + 1) * P], probs[b][:, j, :], ident[:])
                        attended.filled(last, key)

                    elif kind == "values":
                        key = ("values", block, s, i)
                        attended.wait_before(pe, it, key)
                        attended.wait_copied(pe, it, ("turn", block, s, i))
                        b = unit_no[block, s, i] % 2
                        bank = attended.bank(key)
                        if block == "fuse":
                            last = mm(bank[:, 0:D], probsT[b][:, 0, :], mem[s], start=True, stop=True)
                        else:
                            h = HEAD[block]
                            for j in range(GROUP):
                                c = (i * GROUP + j) * h
                                last = mm(bank[:, j * h:(j + 1) * h], probsT[b][:, j, :], vals[s][:, c:c + h], start=True, stop=True)
                                if block == "three" and i == UNITS - 1 and j == 0:
                                    last.then_inc(s_side_used[s], 1)
                        attended.filled(last, key)

                    elif kind == "mcT":
                        key, bank = fill(kind, block, s, 0)
                        attended.wait_copied(pe, it, ("values", "fuse", s, 0))
                        for c in range(DC):
                            last = nc.tensor.transpose(bank[:, c * P:(c + 1) * P], context[s][:, c * P:(c + 1) * P], ident[:])
                        products.filled(last, key)

                    elif kind == "gate":
                        have("fuse")
                        pe.wait_ge(s_bias, 6)
                        key, bank = fill(kind, block, s, 0)
                        copied(("mcT", block, s, 0))
                        mm(bank[:, 0:D], ones_bf[:], bias_parts[:], start=True, stop=False)
                        for c in range(2 * DC):
                            lhs = x_inT[s][:, c, :] if c < DC else contextT[s][:, c - DC, :]
                            last = mm(bank[:, 0:D], lhs, w["gate"][:, c, :], start=False, stop=(c == 2 * DC - 1))
                        products.filled(last, key)

                    elif kind == "kv":
                        wkv = w[block + "_kv"]
                        have("one_kv" if block == "one" else "three")
                        key, bank = fill(kind, block, s, i)
                        if i % 2 == 0:
                            for j in range(4):
                                t = 2 * i + j
                                last = mm(bank[:, j * P:(j + 1) * P], wkv[:, t * P:(t + 1) * P], ctxT[s][:], start=True, stop=True)
                        else:
                            c = INNER + (i // 2) * 512
                            last = mm(bank[:], ctxT[s][:], wkv[:, c:c + 512], start=True, stop=True)
                        products.filled(last, key)

                    elif kind == "nT":
                        key, bank = fill(kind, block, s, 0)
                        pe.wait_ge(s_xn, it * len(xn_no) + xn_no[block, s] + 1)
                        nv = 2 if block == "self" else 1
                        for c in range(DC):
                            for v in range(nv):
                                last = nc.tensor.transpose(bank[:, (c * nv + v) * P:(c * nv + v + 1) * P],
                                                           xn[s][:, v, c * P:(c + 1) * P], ident[:])
                                if block == "one" and c == 0:
                                    last.then_inc(s_x_used[s], 1)
                        products.filled(last, key)

                    elif kind in ("q", "ff1"):
                        name = block + ("_q" if kind == "q" else "_1")
                        have({"one_q": "one", "one_1": "one_ff"}.get(name, "three"))
                        key, bank = fill(kind, block, s, i)
                        copied(("nT", block + ("_ff" if kind == "ff1" else ""), s, 0))
                        for j in range(4):
                            t = 4 * i + j
                            for c in range(DC):
                                last = mm(bank[:, j * P:(j + 1) * P], w[name][:, c, t * P:(t + 1) * P], xnT[s][:, c, 0, :],
                                          start=(c == 0), stop=(c == DC - 1))
                        products.filled(last, key)

                    elif kind == "qkv":
                        have("two_a")
                        key, bank = fill(kind, block, s, i)
                        copied(("nT", block, s, 0))
                        c0, n = ((0, 2 * D), (2 * D, D))[i]
                        k = 0
                        for v, name in enumerate(("v_qkv", "l_qkv")):
                            for c in range(DC):
                                last = mm(bank[:, 0:n], xnT[s][:, c, v, :], w[name][:, c, c0:c0 + n], start=(k == 0), stop=(k == 3))
                                k += 1
                        products.filled(last, key)

                    elif kind == "qkT":
                        key, bank = fill(kind, block, s, i)
                        pe.wait_ge(s_roped, it * SLOTS + roped_no[s] + 1)
                        for j, c in enumerate((0, 1) if i == 0 else (1 + i,)):
                            last = nc.tensor.transpose(bank[:, j * P:(j + 1) * P], roped[s][:, c * P:(c + 1) * P], ident[:])
                        products.filled(last, key)

                    elif kind == "ckv":
                        key, bank = fill(kind, block, s, i)
                        if i == 0:
                            last = mm(bank[:, 0:P], w["ckv"][:, 0:P], ctxT[s][:], start=True, stop=True)
                        else:
                            last = mm(bank[:, 0:P], ctxT[s][:], w["ckv"][:, P:2 * P], start=True, stop=True)
                        products.filled(last, key)

                    elif kind == "cq":
                        key, bank = fill(kind, block, s, 0)
                        copied(("nT", block, s, 0))
                        for c in range(DC):
                            last = mm(bank[:, 0:P], w["cq"][:, c, :], xnT[s][:, c, 0, :], start=(c == 0), stop=(c == DC - 1))
                        products.filled(last, key)

                    elif kind == "oT":
                        n = HEAD[block] * HEADS // P
                        attended.wait_copied(pe, it, ("values", block, s, UNITS - 1 if n <= 4 else (i + 1) * UNITS // 2 - 1))
                        key, bank = fill(kind, block, s, i)
                        for j in range(min(4, n)):
                            t = 4 * i + j
                            last = nc.tensor.transpose(bank[:, j * P:(j + 1) * P], heads[s][:, t * P:(t + 1) * P], ident[:])
                        products.filled(last, key)

                    elif kind in ("wo", "ff2"):
                        key, bank = fill(kind, block, s, 0)
                        if kind == "wo":
                            n = HEAD[block] * HEADS // P
                            have({"one": "one", "three": "three"}.get(block, "two_a"))
                            source = ("oT", block, s)
                            weight = {"self": w["vl_dense"], "cross": w["cdense"][:].unsqueeze(1)}.get(block)
                            weight = w[block + "_o"] if weight is None else weight
                            lhs = [queries[s][:, t * P:(t + 1) * P] for t in range(n)]
                        else:
                            n = IC
                            have({"one": "one_ff"}.get(block, "three"))
                            source = ("ff1", block, s)
                            weight = w[block + "_2"]
                            lhs = [hidden[s][:, t, :] for t in range(n)]
                        width = 2 * D if block == "self" else D
                        for t in range(n):
                            if t % 4 == 0:
                                copied((*source, t // 4))
                            last = mm(bank[:, 0:width], lhs[t], weight[:, t, :], start=(t == 0), stop=(t == n - 1))
                        products.filled(last, key)

                    elif kind == "gu":
                        have("two_mlp")
                        key, bank = fill(kind, block, s, i)
                        copied(("nT", block, s, 0))
                        n = min(2, FC - 2 * i)
                        for g, name in enumerate(("mlp_gate", "mlp_up")):
                            for j in range(n):
                                t = 2 * i + j
                                for c in range(DC):
                                    last = mm(bank[:, (2 * g + j) * P:(2 * g + j + 1) * P], w[name][:, c, t * P:(t + 1) * P],
                                              xnT[s][:, c, 0, :], start=(c == 0), stop=(c == DC - 1))
                        products.filled(last, key)

                    elif kind == "down":
                        key, bank = fill(kind, block, s, 0)
                        copied(("gu", block, s, -(-FC // 2) - 1))
                        mm(bank[:], hidden2[s][:, 0, :], w["down_rest"][:], start=True, stop=False)
                        for t in range(2 * FFULL):
                            e = t // FFULL
                            last = mm(bank[:, e * D:(e + 1) * D], hidden2[s][:, 1 + t, :], w["down"][:, t, :],
                                      start=False, stop=(t == 2 * FFULL - 1))
                        products.filled(last, key)

        @block_.scalar
        def _(act):
            for dst, src in TABLES:
                act.dma_start(dst, src).then_inc(s_tables, 16)
            for dst, src in CONSTS:
                act.dma_start(dst, src).then_inc(s_consts, 16)
            act.wait_ge(s_tables, 16 * len(TABLES))
            act.wait_ge(s_consts, 16 * len(CONSTS))
            nc.scalar.activation(tanh_gates[:], gates[:], ACT.Tanh).then_inc(s_tanh_gates, 1)

            with act.Fori(0, ITERATIONS) as it:
                for kind, block, s, i in STEPS:
                    if kind == "mem":
                        key = (kind, block, s, 0)
                        products.wait_full(act, it, key)
                        bank = products.bank(key)
                        nc.scalar.activation(memT[s], bank[:, 0:D].rearrange("p (c n) -> p c n", c=DC), ACT.Copy, scale=D ** -0.5)
                        products.empty(nc.scalar.activation(mem[s], bank[:, D:2 * D], ACT.Copy), key)

                    elif kind == "scores":
                        key = (block, s, i)
                        n = unit_no[key]
                        act.wait_ge(s_max, it * N_UNITS + n + 1)
                        for before in still_to_come("scores", "turn", key):
                            attended.wait_full(act, it, before)
                        b = n % 2
                        for j in range(1 if block == "fuse" else GROUP):
                            last = nc.scalar.activation(probs[b][:, j, :], scores.bank(key)[:, j * P:(j + 1) * P], ACT.Exp,
                                                        bias=minus_max[:, n, j:j + 1], accum_out=total[:, n, j:j + 1])
                        scores.empty(last, key)

                    elif kind == "mcT":
                        key = (kind, block, s, 0)
                        products.wait_full(act, it, key)
                        products.empty(nc.scalar.activation(contextT[s], products.bank(key)[:, 0:D].rearrange("p (c n) -> p c n", c=DC),
                                                            ACT.Copy), key)

                    elif kind == "gate":
                        key = (kind, block, s, 0)
                        products.wait_full(act, it, key)
                        products.empty(nc.scalar.activation(gate_tanh[s], products.bank(key)[:, 0:D], ACT.Tanh, scale=0.5), key)

                    elif COPIED_BY.get((kind, block, s, i)) == "s":
                        copy_out(act, it, kind, block, s, i)

                    elif kind == "ff1":
                        key = (kind, block, s, i)
                        products.wait_full(act, it, key)
                        products.empty(nc.scalar.activation(hidden[s][:, 4 * i:4 * i + 4, :], products.bank(key)[:].rearrange("p (c n) -> p c n", c=4),
                                                            ACT.Gelu), key)

                    elif kind == "gu":
                        key = (kind, block, s, i)
                        products.wait_full(act, it, key)
                        n = min(2, FC - 2 * i) * P
                        nc.scalar.activation(silu[s][i % len(silu[s])][:, 0:n], products.bank(key)[:, 0:n], ACT.Silu).then_inc(s_silu, 1)

        @block_.vector
        def _(dve):
            state = {"n": 0, "it": 0}

            def link(ins):
                state["n"] += 1
                ins.then_inc(s_link, 1)
                dve.wait_ge(s_link, state["it"] * N_LINKS + SETUP_LINKS + state["n"])

            SETUP_LINKS = 4
            nc.vector.memset(ones_bf[:], 1.0)
            dve.wait_ge(s_tables, 16 * len(TABLES))

            def setup_link(ins, n):
                ins.then_inc(s_link, 1)
                dve.wait_ge(s_link, n)

            setup_link(nc.vector.tensor_scalar(tmp_pos[:, 1, :], positions, 0.0, float(P), ALU.is_lt, ALU.mult), 1)
            setup_link(nc.vector.tensor_tensor(tmp_pos[:, 0, :], positions, tmp_pos[:, 1, :], ALU.add), 2)
            setup_link(nc.vector.tensor_scalar(tmp_pos[:, 1, :], tmp_pos[:, 0, :], 0.0, float(P - 1), ALU.max, ALU.min), 3)
            setup_link(nc.vector.tensor_scalar(tmp_pos[:, 0, :], tmp_pos[:, 1, :], row_number[:, 0:1], None, ALU.is_equal), 4)
            nc.vector.tensor_copy(tmp_pos[:, 1, :], tmp_pos[:, 0, :]).then_inc(s_onehot, 1)
            nc.vector.tensor_copy(ident_bf[:], ident[:])
            nc.vector.tensor_copy(causal[:], causal_f)
            dve.wait_ge(s_rope_full, 1)
            nc.vector.tensor_copy(rope[:], attended.banks[0][:, 0:32]).then_inc(s_rope, 1)
            dve.wait_ge(s_rope, 1)
            dve.wait_ge(s_set, 1)
            dve.wait_ge(s_consts, 16 * len(CONSTS))
            dve.wait_ge(s_tanh_gates, 1)

            with dve.Fori(0, ITERATIONS) as it:
                state["it"] = it
                state["n"] = 0

                def statistics(name, s):
                    n = norm_no[name, s]
                    nc.vector.bn_stats(moments[:, n, :], x[s][:])
                    dve.drain()
                    link(nc.vector.bn_aggr(mean_var[:, n, :], moments[:, n, :]))
                    mean, var = mean_var[:, n, 0:1], mean_var[:, n, 1:2]
                    if name not in CENTRED:
                        link(nc.vector.scalar_tensor_tensor(out=square[:, n:n + 1], in0=mean, scalar=mean, in1=var, op0=ALU.mult, op1=ALU.add))
                        var = square[:, n:n + 1]
                    nc.vector.tensor_scalar(var_eps[:, n:n + 1], var, EPS[name], None, ALU.add).then_inc(s_var, 1)

                def normalise(name, s):
                    n = norm_no[name, s]
                    dve.wait_ge(s_rstd, it * N_NORMS + n + 1)
                    r = rstd[:, n:n + 1]
                    if name == "fuse":
                        link(nc.vector.scalar_tensor_tensor(out=x[s][:], in0=x[s][:], scalar=r, in1=fuse_gain[:], op0=ALU.mult, op1=ALU.mult))
                    elif name == "self":
                        for v in range(2):
                            link(nc.vector.tensor_scalar(rstd_expert[:, s, v:v + 1], r, expert[s][:, v:v + 1], None, ALU.mult))
                        nc.vector.tensor_scalar(xn[s][:, 0, :], x[s][:], rstd_expert[:, s, 0:1], None, ALU.mult)
                        nc.vector.tensor_scalar(xn[s][:, 1, :], x[s][:], rstd_expert[:, s, 1:2], None, ALU.mult).then_inc(s_xn, 1)
                    elif name in CENTRED:
                        nc.vector.tensor_scalar(xn[s][:, 0, :], x[s][:], mean_var[:, n, 0:1], r, ALU.subtract, ALU.mult).then_inc(s_xn, 1)
                    else:
                        nc.vector.tensor_scalar(xn[s][:, 0, :], x[s][:], r, None, ALU.mult).then_inc(s_xn, 1)

                for kind, block, s, i in STEPS:
                    if kind == "mem":
                        dve.wait_ge(s_side[s], (it + 1) * 48)
                        nc.vector.tensor_scalar(keep[s][:], keep_in[s][:], 1.0, -MASKED, ALU.subtract, ALU.mult).then_inc(s_keep, 1)
                        link(nc.vector.tensor_scalar(expert[s][:, 2:4], types[s][:], 1.0, None, ALU.is_equal))
                        link(nc.vector.tensor_tensor(expert[s][:, 0:1], expert[s][:, 2:3], expert[s][:, 3:4], ALU.mult))
                        nc.vector.tensor_scalar(expert[s][:, 1:2], expert[s][:, 0:1], -1.0, 1.0, ALU.mult, ALU.add)

                    elif kind == "scores":
                        key = (block, s, i)
                        n = unit_no[key]
                        g = 1 if block == "fuse" else GROUP
                        scores.wait_full(dve, it, key)
                        nc.vector.tensor_reduce(minus_max[:, n, 0:g], scores.bank(key)[:, 0:g * P].rearrange("p (h k) -> p h k", h=g),
                                                AX.X, ALU.max, negate=True).then_inc(s_max, 1)

                    elif COPIED_BY.get((kind, block, s, i)) == "v":
                        copy_out(dve, it, kind, block, s, i)

                    elif kind == "values":
                        key = ("values", block, s, i)
                        n = unit_no[block, s, i]
                        g = 1 if block == "fuse" else GROUP
                        attended.wait_full(dve, it, key)
                        link(nc.vector.reciprocal(inv_total[:, n, 0:g], total[:, n, 0:g]))
                        if block == "fuse":
                            ins = nc.vector.tensor_scalar(context[s], attended.bank(key)[:, 0:D], inv_total[:, n, 0:1], None, ALU.mult)
                        else:
                            h = HEAD[block]
                            c = i * GROUP * h
                            ins = nc.vector.tensor_tensor(heads[s][:, c:c + GROUP * h].rearrange("p (g h) -> p g h", g=GROUP),
                                                          attended.bank(key)[:, 0:GROUP * h].rearrange("p (g h) -> p g h", g=GROUP),
                                                          inv_total[:, n, :].unsqueeze(2).to_broadcast([P, GROUP, h]), ALU.mult)
                        attended.empty(ins, key)

                    elif kind == "gate":
                        products.wait_emptied(dve, it, (kind, block, s, 0))
                        link(nc.vector.scalar_tensor_tensor(out=gated[s], in0=gate_tanh[s], scalar=1.0, in1=context[s], op0=ALU.add, op1=ALU.mult))
                        dve.wait_ge(s_x_free[s], it + 1)
                        link(nc.vector.scalar_tensor_tensor(out=x[s][:], in0=gated[s], scalar=0.5, in1=x_in[s][:], op0=ALU.mult, op1=ALU.add))

                    elif kind == "qkv" and i == 0:
                        key = (kind, block, s, 0)
                        products.wait_full(dve, it, key)
                        qk = products.bank(key)[:].rearrange("p (h r) -> p h r", r=16)
                        ra, rb = (t[s].rearrange("p (h r) -> p h r", r=16) for t in (rope_a, rope_b))
                        nc.vector.tensor_tensor(ra, qk, rope[:, 0:16].unsqueeze(1).to_broadcast([P, 32, 16]), ALU.mult)
                        nc.vector.tensor_tensor(rb[:, :, 0:8], qk[:, :, 8:16], rope[:, 16:24].unsqueeze(1).to_broadcast([P, 32, 8]), ALU.mult)
                        ins = nc.vector.tensor_tensor(rb[:, :, 8:16], qk[:, :, 0:8], rope[:, 24:32].unsqueeze(1).to_broadcast([P, 32, 8]), ALU.mult)
                        products.empty(ins, key)
                        products.wait_emptied(dve, it, key)
                        nc.vector.tensor_tensor(roped[s], rope_a[s], rope_b[s], ALU.add).then_inc(s_roped, 1)

                    elif kind == "qkT" and i > 0 or kind == "ckv" and i == 0:
                        key = (kind, block, s, i)
                        products.wait_full(dve, it, key)
                        first, n, col = (2, 8, (i - 1) * 8 * P) if kind == "qkT" else (10, 16, 0)
                        products.empty(nc.vector.tensor_tensor(
                            keys[s][:, col:col + n * P].rearrange("p (h n) -> p h n", h=n),
                            products.bank(key)[:, 0:P].unsqueeze(1).to_broadcast([P, n, P]),
                            member[:, first:first + n].unsqueeze(2).to_broadcast([P, n, P]), ALU.mult), key)

                    elif kind in ("wo", "ff2", "down"):
                        key = (kind, block, s, 0)
                        products.wait_full(dve, it, key)
                        bank = products.bank(key)
                        if block in ("one", "three"):
                            g = GATES.index(block + ("_ff" if kind == "ff2" else ""))
                            ins = nc.vector.scalar_tensor_tensor(out=x[s][:], in0=bank[:, 0:D], scalar=tanh_gates[:, g:g + 1], in1=x[s][:],
                                                                 op0=ALU.mult, op1=ALU.add)
                        elif block == "cross":
                            ins = nc.vector.tensor_tensor(x[s][:], bank[:, 0:D], x[s][:], ALU.add)
                        else:
                            link(nc.vector.scalar_tensor_tensor(out=x[s][:], in0=bank[:, 0:D], scalar=expert[s][:, 0:1], in1=x[s][:],
                                                                op0=ALU.mult, op1=ALU.add))
                            ins = nc.vector.scalar_tensor_tensor(out=x[s][:], in0=bank[:, D:2 * D], scalar=expert[s][:, 1:2], in1=x[s][:],
                                                                 op0=ALU.mult, op1=ALU.add)
                        products.empty(ins, key)
                        if (kind, block) in STATISTICS:
                            products.wait_emptied(dve, it, key)

                    elif kind == "xn":
                        normalise(block, s)

                    elif kind == "gu":
                        key = (kind, block, s, i)
                        dve.wait_ge(s_silu, it * len(gu_no) + gu_no[s, i] + 1)
                        n = min(2, FC - 2 * i) * P
                        products.empty(nc.vector.tensor_tensor(keys[s][:, 2 * i * P:2 * i * P + n], products.bank(key)[:, 2 * P:2 * P + n],
                                                               silu[s][i % len(silu[s])][:, 0:n], ALU.mult), key)
                    if (kind, block) in STATISTICS:
                        statistics(STATISTICS[kind, block], s)
                assert state["n"] == N_LINKS, (state["n"], N_LINKS)


def kernel(**inputs):
    import numpy as _np
    import concourse.bacc as _bacc
    from concourse import mybir as _mybir
    from concourse.bass_utils import run_bass_kernel_spmd as _run

    a = {name: _np.asarray(v) for name, v in inputs.items()}

    def by_chunk(m):
        return m.reshape(-1, P, m.shape[1]).transpose(1, 0, 2)

    L0, L1, L2, L3 = (f"L{i}_xattn_" for i in range(4))
    arrays = {
        "x": a["x"],
        "xT": a["x"].reshape(BATCH, P, DC, P).transpose(0, 3, 2, 1),
        "ctxT": a["ctx_1024"].transpose(0, 2, 1),
        "keep": a["mask_BxS2_bk0"],
        "types": _np.stack([a["mask_BxS_ik0"], _np.pad(a["mask_BxS_ik0"][:, 1:], ((0, 0), (0, 1)))], axis=2),
        "positions": a["pos_1xS"],
        "mem": a[L0 + "W_mem"].T, "gate": by_chunk(a[L0 + "W_gate"].T),
        "fuse_gain": a[L0 + "norm_w"][None],
        "gates": _np.concatenate([a[L1 + "attn_gate"], a[L1 + "ff_gate"], a[L3 + "attn_gate"], a[L3 + "ff_gate"]])[None],
        "v_qkv": by_chunk(a[L2 + "v_qkv"]), "l_qkv": by_chunk(a[L2 + "l_qkv"]),
        "vl_dense": by_chunk(_np.concatenate([a[L2 + "v_dense"], a[L2 + "l_dense"]], axis=1)),
        "cq": by_chunk(a[L2 + "cq_w"]), "ckv": a[L2 + "ckv_w"], "cdense": a[L2 + "cdense_w"],
    }
    arrays["gate_bias"] = _np.zeros((P, D), _np.float32)
    arrays["gate_bias"][0:96:32] = a[L0 + "b_gate"]
    for name, pre in (("one", L1), ("three", L3)):
        arrays[name + "_q"] = by_chunk(a[pre + "Wq"])
        arrays[name + "_kv"] = a[pre + "Wkv"]
        arrays[name + "_o"] = by_chunk(a[pre + "Wo"])
        arrays[name + "_1"] = by_chunk(a[pre + "W1"])
        arrays[name + "_2"] = by_chunk(a[pre + "W2"])
    full, half = FFULL * P, P // 2
    for name in ("gate", "up"):
        v, l = a[f"{L2}v_{name}"], a[f"{L2}l_{name}"]
        rest = [_np.pad(m[:, full:], ((0, 0), (0, half - FREST))) for m in (v, l)]
        arrays["mlp_" + name] = by_chunk(_np.concatenate([*rest, v[:, :full], l[:, :full]], axis=1))
    v, l = a[L2 + "v_down"], a[L2 + "l_down"]
    arrays["down_rest"] = _np.concatenate([_np.pad(v[full:], ((0, half - FREST), (0, D))), _np.pad(l[full:], ((0, half - FREST), (D, 0)))])
    arrays["down"] = by_chunk(_np.concatenate([v[:full], l[:full]]))
    gains = [(L1 + "ln_q_g", L1 + "ln_q_b"), (L1 + "ln_ff_g", L1 + "ln_ff_b"), (L2 + "ln_in_w",) * 2, (L2 + "ln_post_cross_w",) * 2,
             (L2 + "ln_post_attn_w",) * 2, (L3 + "ln_q_g", L3 + "ln_q_b"), (L3 + "ln_ff_g", L3 + "ln_ff_b")]
    features = _np.stack([_np.stack([a[n].reshape(DC, P) for n in pair]) for pair in gains]).transpose(3, 0, 1, 2).reshape(P, -1)
    rows = _np.arange(P)
    member = [(rows[:, None] // width == _np.arange(P // width)).astype(_np.float32) for width in (64, 16, 8)]
    arrays["table"] = _np.concatenate([features, _np.eye(P, dtype=_np.float32), *member, rows[:, None].astype(_np.float32)], axis=1)
    causal = _np.where(rows[:, None] >= rows, 0.0, MASKED).astype(_np.float32)
    inverse = (1.0 / 10000.0 ** (_np.arange(0, 16, 2, dtype=_np.float32) / 16)).astype(_np.float32)
    angle = rows[:, None].astype(_np.float32) * inverse
    arrays["causal_rope"] = _np.concatenate([causal, _np.cos(angle), _np.cos(angle), -_np.sin(angle), _np.sin(angle)],
                                            axis=1).astype(_np.float32)

    nc = _bacc.Bacc("TRN2", target_bir_lowering=False, num_devices=1)
    given, aps = {}, {}
    for name, v in arrays.items():
        given["in_" + name] = _np.ascontiguousarray(v)
        aps[name] = nc.dram_tensor("in_" + name, v.shape, _mybir.dt.from_np(v.dtype), kind="ExternalInput").ap()
    out = nc.dram_tensor("out", a["x"].shape, _mybir.dt.float32, kind="ExternalOutput").ap()
    build(nc, aps, out)
    r = _run(nc, [given], core_ids=[0])
    return r.results[0]["out"]
```
